# Optimizing a Trainium2 kernel written in Bass

```python
import numpy as np
import jax
import jax.numpy as jnp

def _softmax(x, axis=-1):
    return jax.nn.softmax(x, axis=axis)

def _gelu(x):
    return jax.nn.gelu(x, approximate=True)

def _silu(x):
    return jax.nn.silu(x)

def _sigmoid(x):
    return jax.nn.sigmoid(x)

def _layernorm(x, axis=-1, eps=1e-05):
    m = jnp.mean(x, axis=axis, keepdims=True)
    v = jnp.var(x, axis=axis, keepdims=True)
    return (x - m) / jnp.sqrt(v + eps)

def _scatter_add(tgt, idx, src, axis=0):
    return tgt.at[idx].add(src)

def _segment_sum(src, seg, n):
    return jax.ops.segment_sum(src, seg, n)
kernel_name = 'mk_macaron_d1_jaxref_r8_c8e35f'

def setup_inputs(seed: int=0):
    np.random.seed(seed)
    _w = jnp.asarray

    def _L0_attn_setup():
        import jax, jax.numpy as jnp
        import numpy as np
        DIM = 128

        def _circ_conv(x, key):
            D = x.shape[-1]
            return jnp.fft.irfft(jnp.fft.rfft(x, axis=-1) * jnp.fft.rfft(key), n=D, axis=-1)

        def _circ_corr(x, key):
            D = x.shape[-1]
            return jnp.fft.irfft(jnp.fft.rfft(x, axis=-1) * jnp.conj(jnp.fft.rfft(key)), n=D, axis=-1)
        key = jax.random.key(seed)
        k0, k1, k2 = jax.random.split(key, 3)
        B, T, D = (4, 256, DIM)
        x = jax.random.normal(k0, (B, T, D), dtype=jnp.float32)
        bind_key = jax.random.normal(k1, (D,), dtype=jnp.float32) * 0.02
        unbind_key = jax.random.normal(k2, (D,), dtype=jnp.float32) * 0.02
        gate = jnp.ones((1,), dtype=jnp.float32)
        decay = jnp.asarray(0.9, dtype=jnp.float32)
        return {'x': x, 'bind_key': bind_key, 'unbind_key': unbind_key, 'gate': gate, 'decay': decay}
    _L0_attn_in = _L0_attn_setup()

    def _L0_ffn_setup():
        import jax, jax.numpy as jnp
        import numpy as np
        B, T, C, H, E = (1, 32, 128, 256, 8)
        STD = 0.02
        key = jax.random.key(seed)
        ks = jax.random.split(key, 8)
        f32 = jnp.float32
        return {'x': jax.random.normal(ks[0], (B, T, C), f32), 'up': jax.random.normal(ks[1], (E, H, C), f32) * STD, 'gate': jax.random.normal(ks[2], (E, H, C), f32) * STD, 'down': jax.random.normal(ks[3], (E, C, H), f32) * STD, 'router': jax.random.normal(ks[4], (E, C), f32) * STD, 'w_up_s': jax.random.normal(ks[5], (H, C), f32) * STD, 'w_gate_s': jax.random.normal(ks[6], (H, C), f32) * STD, 'w_down_s': jax.random.normal(ks[7], (C, H), f32) * STD}
    _L0_ffn_in = _L0_ffn_setup()
    _d = {'L0_attn_x': _L0_attn_in['x'], 'L0_attn_bind_key': _L0_attn_in['bind_key'], 'L0_attn_unbind_key': _L0_attn_in['unbind_key'], 'L0_attn_gate': _L0_attn_in['gate'], 'L0_attn_decay': _L0_attn_in['decay'], 'L0_ffn_up': _L0_ffn_in['up'], 'L0_ffn_gate': _L0_ffn_in['gate'], 'L0_ffn_down': _L0_ffn_in['down'], 'L0_ffn_router': _L0_ffn_in['router'], 'L0_ffn_w_up_s': _L0_ffn_in['w_up_s'], 'L0_ffn_w_gate_s': _L0_ffn_in['w_gate_s'], 'L0_ffn_w_down_s': _L0_ffn_in['w_down_s']}
    _x0 = _d['L0_attn_x']
    _d['L0_attn_x'] = jax.random.normal(jax.random.fold_in(jax.random.key(seed), 1), (16, 256, 128), dtype=_x0.dtype)
    del _x0
    return _d

def reference(L0_attn_x, L0_attn_bind_key, L0_attn_unbind_key, L0_attn_gate, L0_attn_decay, L0_ffn_up, L0_ffn_gate, L0_ffn_down, L0_ffn_router, L0_ffn_w_up_s, L0_ffn_w_gate_s, L0_ffn_w_down_s):

    def _L0_attn_ref(x, bind_key, unbind_key, gate, decay):
        import jax, jax.numpy as jnp
        import numpy as np
        DIM = 128

        def _circ_conv(x, key):
            D = x.shape[-1]
            return jnp.fft.irfft(jnp.fft.rfft(x, axis=-1) * jnp.fft.rfft(key), n=D, axis=-1)

        def _circ_corr(x, key):
            D = x.shape[-1]
            return jnp.fft.irfft(jnp.fft.rfft(x, axis=-1) * jnp.conj(jnp.fft.rfft(key)), n=D, axis=-1)
        B, T, D = x.shape
        bound = _circ_conv(x, bind_key)
        d = jax.nn.sigmoid(decay)
        pos = jnp.arange(T, dtype=x.dtype)
        diff = pos[:, None] - pos[None, :]
        causal = diff >= 0
        decay_matrix = jnp.where(causal, d ** jnp.maximum(diff, 0.0), 0.0)
        hologram = jnp.einsum('ts,bsd->btd', decay_matrix, bound)
        retrieved = _circ_corr(hologram, unbind_key)
        return x + gate * retrieved

    def _L0_ffn_ref(x, up, gate, down, router, w_up_s, w_gate_s, w_down_s):
        import jax, jax.numpy as jnp
        import numpy as np
        B, T, C, H, E = (1, 32, 128, 256, 8)
        STD = 0.02
        b, t, c = x.shape
        x_ = x.reshape(b * t, c)
        logits = x_ @ router.T
        idx = jnp.argmax(logits, axis=-1)
        onehot = jax.nn.one_hot(idx, router.shape[0], dtype=x.dtype)
        u = jnp.einsum('bc,ehc->ebh', x_, up)
        g = jnp.einsum('bc,ehc->ebh', x_, gate)
        h = jax.nn.silu(g) * u
        ye = jnp.einsum('ebh,ech->ebc', h, down)
        y = jnp.einsum('ebc,be->bc', ye, onehot)
        ys = jax.nn.silu(x_ @ w_gate_s.T) * (x_ @ w_up_s.T) @ w_down_s.T
        return (y + ys).reshape(b, t, c)
    x = L0_attn_x
    x = x + 0.5 * _L0_ffn_ref(_layernorm(x, axis=-1), L0_ffn_up, L0_ffn_gate, L0_ffn_down, L0_ffn_router, L0_ffn_w_up_s, L0_ffn_w_gate_s, L0_ffn_w_down_s)
    x = x + _L0_attn_ref(_layernorm(x, axis=-1), L0_attn_bind_key, L0_attn_unbind_key, L0_attn_gate, L0_attn_decay)
    x = x + 0.5 * _L0_ffn_ref(_layernorm(x, axis=-1), L0_ffn_up, L0_ffn_gate, L0_ffn_down, L0_ffn_router, L0_ffn_w_up_s, L0_ffn_w_gate_s, L0_ffn_w_down_s)
    return x

_drawn_inputs = setup_inputs


def setup_inputs(seed=0):
    import zlib

    import numpy as np

    out = dict(_drawn_inputs(seed))
    spreads = {}
    factors = {'L0_ffn_up': 8.0,
     'L0_ffn_gate': 8.0,
     'L0_ffn_down': 8.0,
     'L0_ffn_router': 8.0,
     'L0_ffn_w_up_s': 8.0,
     'L0_ffn_w_gate_s': 8.0,
     'L0_ffn_w_down_s': 8.0}
    for name, (base, spread) in spreads.items():
        noise = np.random.default_rng([zlib.crc32(name.encode()), seed]).standard_normal(out[name].shape)
        drawn = base * np.exp(spread * noise) if base else spread * noise
        out[name] = jnp.asarray(drawn.astype(out[name].dtype))
    for name, factor in factors.items():
        out[name] = (out[name] * factor).astype(out[name].dtype)
    return out
```

```python
from contextlib import ExitStack

import concourse.bass as bass
from concourse import mybir

ALU = mybir.AluOpType
ACT = mybir.ActivationFunctionType
AX = mybir.AxisListType
F32 = mybir.dt.float32
BF16 = mybir.dt.bfloat16
I32 = mybir.dt.int32

P = 128
C = 128
E = 8
SHARED = E
H = 256
HH = H // P
B, T = 16, 256
N = B * T
NT = N // P
TPG = 4
G = NT // TPG
GC = TPG * P
ROW = C + 4
CAP = N + P
NB = NT + E - 1
NBL = NB + 1
BU = 8
PAIRS = BU // 2
DUMP = N + E * P
EPS = 1e-05


LOADS = NBL // BU
ROUTE_STEPS = 9
RSTD_STEPS = 4
TAB_STEPS = 19
N_CONST = 15 + BU


def slot_blocks(s):
    return len(range(s, NB, BU))


def pipeline(eng, body, first, last, loop_from, loops, unroll):
    for k in range(first, loop_from):
        body(k, k)
    with eng.Fori(0, loops) as i:
        for u in range(unroll):
            body(loop_from + u + i * unroll, loop_from + u)
    for k in range(loop_from + loops * unroll, last + 1):
        body(k, k)


def ahead(j, s):
    return not isinstance(j, int) or j * BU + s + 3 < NBL


def with_blocks(eng, step):
    for s in range(BU):
        step(0, s)
    with eng.Fori(1, NB // BU) as j:
        for s in range(BU):
            step(j, s)
    for b in range(NB // BU * BU, NB):
        step(b // BU, b % BU, more=b + 1 < NB)


def build(nc, x_in, gu_in, dn_in, router_in, bind_in, unbind_in, gate_in, decay_in, out):
    x_dram = x_in.rearrange("b t c -> (b t) c").rearrange("(i p) c -> p i c", p=P)
    out_dram = out.rearrange("b t c -> (b t) c").rearrange("(i p) c -> p i c", p=P)
    dispatched = nc.dram_tensor("dispatched", [E * CAP, ROW], F32, kind="Internal")
    returned = nc.dram_tensor("returned", [DUMP * (E + 1), C], F32, kind="Internal")
    returned_tiles = returned[0:N, :].rearrange("(i p) c -> p i c", p=P)

    with ExitStack() as ctx:
        def sb(name, shape, dt=F32):
            return ctx.enter_context(nc.sbuf_tensor(name, shape, dt))

        def sem(name):
            return ctx.enter_context(nc.semaphore(name))

        gu = sb("gu", [P, E + 1, 2 * H])
        dn = sb("dn", [P, E + 1, HH, C])
        routerT = sb("routerT", [P, E])
        ident = sb("ident", [P, P])
        before = sb("before", [P, P], BF16)
        ones = sb("ones", [P, P], BF16)
        region = sb("region", [P, TPG * E])
        prefer = sb("prefer", [P, TPG * E])
        pad_base = sb("pad_base", [P, E])
        upto = sb("upto", [P, E, E])
        block_no = sb("block_no", [P, NBL])
        minus_half = sb("minus_half", [P, TPG])
        minus_one = sb("minus_one", [P, TPG])
        eps = sb("eps", [P, TPG])
        numbers = sb("numbers", [P, NT], I32)
        pads = sb("pads", [P, E, ROW])
        hank_b = sb("hank_b", [P, P])
        hank_u = sb("hank_u", [P, P])
        mix = sb("mix", [P, C])
        gate = sb("gate", [P, 1])
        decay = sb("decay", [P, 2])
        keep = sb("keep", [P, GC])

        xres = sb("xres", [P, NT, C])
        xn = sb("xn", [P, 2, TPG, ROW])
        xa = sb("xa", [P, 2, TPG, C])
        back = sb("back", [P, 2, TPG, C])
        xnT = sb("xnT", [P, 2, GC])
        scanned = sb("scanned", [P, 2, GC])
        attn_sum = sb("attn_sum", [P, GC])
        st = {k: sb("st_" + k, [P, TPG, 6]) for k in "fa"}
        mv = {k: sb("mv_" + k, [P, 2, TPG, 2]) for k in "fa"}
        var = {k: sb("var_" + k, [P, TPG]) for k in "fa"}
        mr = {k: sb("mr_" + k, [P, TPG]) for k in "fa"}
        scale = {k: sb("scale_" + k, [P, 2, TPG]) for k in "fa"}
        shift = {k: sb("shift_" + k, [P, 2, TPG]) for k in "fa"}

        top = sb("top", [P, TPG])
        cand = sb("cand", [P, TPG, E])
        first = sb("first", [P, TPG])
        chosen = sb("chosen", [P, 2, TPG, E], BF16)
        seen = sb("seen", [P, 2, E], BF16)
        seen_now = sb("seen_now", [P, E])
        place = sb("place", [P, TPG, E])
        slot = sb("slot", [P, 2, TPG], I32)
        pad_row = sb("pad_row", [P, E], I32)
        n_up = sb("n_up", [P, E], I32)
        n_blk = sb("n_blk", [P, E], I32)
        blk = sb("blk", [P, E])
        blk_upto = sb("blk_upto", [P, E, E])
        blk_end = sb("blk_end", [P, E])
        last_blk = sb("last_blk", [P, 1])
        real_blk = sb("real_blk", [P, NBL])
        past = sb("past", [P, NBL, E])
        past_n = sb("past_n", [P, NBL, E])
        blk_exp = sb("blk_exp", [P, 1 + NBL + 1])
        blk_from = sb("blk_from", [P, NBL])
        extra = sb("extra", [P, NBL])
        to_replica = sb("to_replica", [P, NBL], I32)
        digit = sb("digit", [P, BU])
        packed = {u: sb("packed_" + u, [P, LOADS, BU]) for u in ("up", "down")}
        tab_exp = {u: sb("tab_exp_" + u, [P, LOADS], I32) for u in ("up", "down")}
        tab_row = sb("tab_row", [P, NBL], I32)

        sg = sb("sg", [P, HH, GC])
        hs = sb("hs", [P, HH, GC])

        xs = sb("xs", [P, BU, ROW])
        token = sb("token", [P, BU], I32)
        xsT = sb("xsT", [P, 2, 2, P])
        eg = sb("eg", [P, 2, H])
        eh = sb("eh", [P, 2, H])
        ehT = sb("ehT", [P, 2, H])
        ey = sb("ey", [P, BU, C])

        bank = [ctx.enter_context(nc.psum_tensor(f"bank{i}", [P, GC], F32)) for i in range(8)]
        tp = {"f": bank[0], "a": bank[1]}
        rt = bank[2]
        o_ps = bank[3]
        g_ps, u_ps = [bank[4], bank[6]], [bank[5], bank[7]]
        LOG, RANK, TOT = slice(0, 32), slice(32, 64), slice(64, 64 + E)

        const_made = sem("const_made")
        const_chain = sem("const_chain")
        x_in0, x_in1, x_rest = sem("x_in0"), sem("x_in1"), sem("x_rest")
        small_in = sem("small_in")
        shared_in, experts_in = sem("shared_in"), sem("experts_in")
        tanh_done, setup, mix_raw = sem("tanh_done"), sem("setup"), sem("mix_raw")
        bn_done = {k: sem("bn_done_" + k) for k in "fa"}
        stats = {k: sem("stats_" + k) for k in "fa"}
        rstd_done = {k: sem("rstd_done_" + k) for k in "fa"}
        normed = {k: sem("normed_" + k) for k in "fa"}
        turned = {k: sem("turned_" + k) for k in "fa"}
        xnT_ready = sem("xnT_ready")
        logits = sem("logits")
        route = sem("route")
        ranked = sem("ranked")
        slotted = sem("slotted")
        numbered = sem("numbered")
        sent = [sem("sent0"), sem("sent1")]
        gu_done = sem("gu_done")
        silu_done, mult_done = sem("silu_done"), sem("mult_done")
        down_done, half_done = sem("down_done"), sem("half_done")
        totals, tabs, pads_at = sem("totals"), sem("tabs"), sem("pads_at")
        table_ready, pad_sent = sem("table_ready"), sem("pad_sent")
        back_in = [sem("back_in0"), sem("back_in1")]
        x1_done, scan_done, mixed = sem("x1_done"), sem("scan_done"), sem("mixed")
        x2_read, x2_done = sem("x2_read"), sem("x2_done")
        blk_in = [sem(f"blk_in{s}") for s in range(BU)]
        blk_out = [sem(f"blk_out{s}") for s in range(BU)]
        blk_tok = sem("blk_tok")
        blk_turn, blk_xT = sem("blk_turn"), sem("blk_xT")
        blk_gu, blk_silu, blk_mul = sem("blk_gu"), sem("blk_silu"), sem("blk_mul")
        blk_hturn, blk_hT = sem("blk_hturn"), sem("blk_hT")
        blk_dn, blk_y = sem("blk_dn"), sem("blk_y")
        x3_done, stored = sem("x3_done"), [sem("stored0"), sem("stored1")]

        block = ctx.enter_context(nc.Block())

        def tiles(buf, k):
            return buf[:, bass.ds(k * TPG, TPG), :]

        def tile(buf, i):
            return buf[:, bass.ds(i, 1), :].rearrange("p a c -> p (a c)")

        def by_tile(ap):
            return ap.rearrange("p (t e) -> p t e", t=TPG)

        def valid(ks):
            return 0 <= ks < G

        def stand(eng):
            eng.nop(nofuse=True)

        def wait_pos(eng, s, value):
            if not (isinstance(value, int) and value <= 0):
                eng.wait_ge(s, value)

        @block.sync
        def _(sp):
            sp.dma_start(xres[:, 0:TPG, :], x_dram[:, 0:TPG, :]).then_inc(x_in0, 16)
            sp.dma_start(xres[:, TPG:2 * TPG, :], x_dram[:, TPG:2 * TPG, :]).then_inc(x_in1, 16)
            sp.dma_start(routerT[:], router_in).then_inc(small_in, 16)
            sp.dma_start(gu[:, SHARED, :], gu_in[:, SHARED, :]).then_inc(shared_in, 16)
            sp.dma_start(dn[:, SHARED, :, :], dn_in[:, SHARED, :, :]).then_inc(shared_in, 16)
            for key, hank in ((bind_in, hank_b), (unbind_in, hank_u)):
                windows = bass.AP(key.tensor, 0, [[1, P], [1, P]])
                sp.dma_start(hank[:], windows).then_inc(small_in, 16)
            sp.dma_start(gate[:], gate_in.partition_broadcast(P)).then_inc(small_in, 16)
            sp.dma_start(decay[:, 0:1], decay_in.partition_broadcast(P)).then_inc(small_in, 16)
            sp.dma_start(xres[:, 2 * TPG:NT, :], x_dram[:, 2 * TPG:NT, :]).then_inc(x_rest, 16)
            sp.dma_start(gu[:, 0:E, :], gu_in[:, 0:E, :]).then_inc(experts_in, 16)
            sp.dma_start(dn[:, 0:E, :, :], dn_in[:, 0:E, :, :]).then_inc(experts_in, 16)

            def load_block(f, j, s):
                b = j * BU + s
                wait_pos(sp, blk_turn, f * (NBL // 2) + (j - 1) * PAIRS + s // 2 + 1)
                stand(sp)
                first_use = isinstance(j, int) and j == 0
                wait_pos(sp, blk_tok, f * NB if first_use else f * NB + b - BU + 1)
                stand(sp)
                row = sp.value_load(tab_row[0:1, bass.ds(b, 1)], min_val=0, max_val=E * CAP - P)
                sp.dma_start(xs[:, s, :], dispatched[bass.ds(row, P), :]).then_inc(blk_in[s], 16)

            sp.wait_ge(const_made, N_CONST)
            for f in range(2):
                sp.wait_ge(pads_at, f + 1)
                for e in range(E):
                    row = sp.value_load(pad_row[0:1, e:e + 1], min_val=0, max_val=E * CAP - P)
                    sp.dma_start(dispatched[bass.ds(row, P), :], pads[:, e, :]).then_inc(pad_sent, 16)
                sp.wait_ge(table_ready, f + 1)
                sp.wait_ge(pad_sent, 16 * E * (f + 1))
                for q in range(2):
                    sp.wait_ge(sent[q], 16 * TPG * (G // 2) * (f + 1))
                for s in range(BU):
                    load_block(f, 0, s)
                with sp.Fori(1, LOADS) as j:
                    for s in range(BU):
                        load_block(f, j, s)
                for s in range(BU):
                    sp.wait_ge(blk_out[s], 16 * slot_blocks(s) * (f + 1))
                for k in range(G):
                    if k >= 2:
                        sp.wait_ge(x1_done if f == 0 else x3_done, k - 1)
                    sp.dma_start(back[:, k % 2, :, :],
                                 returned_tiles[:, k * TPG:(k + 1) * TPG, :]).then_inc(back_in[k % 2], 16)
                    if f == 1 and k >= 2:
                        sp.dma_start(out_dram[:, (k - 2) * TPG:(k - 1) * TPG, :],
                                     xres[:, (k - 2) * TPG:(k - 1) * TPG, :]).then_inc(stored[k % 2], 16)
            for k in range(G - 2, G):
                sp.wait_ge(x3_done, k + 1)
                sp.dma_start(out_dram[:, k * TPG:(k + 1) * TPG, :],
                             xres[:, k * TPG:(k + 1) * TPG, :]).then_inc(stored[k % 2], 16)
            for q in range(2):
                sp.wait_ge(stored[q], 16 * (G // 2))

        @block.gpsimd
        def _(pool):
            chained = [0]
            small = dict(allow_small_or_imprecise_dtypes=True)

            def chain(ins):
                chained[0] += 1
                ins.then_inc(const_chain, 1)
                pool.wait_ge(const_chain, chained[0])

            chain(nc.gpsimd.memset(ident[:], 0.0))
            nc.gpsimd.affine_select(out=ident[:], in_=ident[:], compare_op=ALU.not_equal, fill=1.0, base=0,
                                    pattern=[[-1, P]], channel_multiplier=1).then_inc(const_made, 1)
            nc.gpsimd.memset(minus_half[:], -0.5).then_inc(const_made, 1)
            nc.gpsimd.memset(minus_one[:], -1.0).then_inc(const_made, 1)
            nc.gpsimd.memset(eps[:], EPS).then_inc(const_made, 1)
            last_row = pool.to_reg(E * CAP - 1)
            last_back = pool.to_reg(DUMP * (E + 1) - 1)

            def rstd(kind, n, q):
                s = rstd_done[kind]
                pool.wait_ge(stats[kind], n + 1)
                wait_pos(pool, normed[kind], n - 1)
                m = mv[kind][:, q, :, :]
                nc.gpsimd.tensor_tensor(var[kind][:], m[:, :, 1], eps[:], ALU.add).then_inc(s, 1)
                pool.wait_ge(s, n * RSTD_STEPS + 1)
                nc.gpsimd.tensor_tensor(scale[kind][:, q, :], var[kind][:], minus_half[:], ALU.pow).then_inc(s, 1)
                pool.wait_ge(s, n * RSTD_STEPS + 2)
                nc.gpsimd.tensor_tensor(mr[kind][:], scale[kind][:, q, :], m[:, :, 0], ALU.mult).then_inc(s, 1)
                pool.wait_ge(s, n * RSTD_STEPS + 3)
                nc.gpsimd.tensor_tensor(shift[kind][:, q, :], mr[kind][:], minus_one[:], ALU.mult).then_inc(s, 1)

            def scatter(f, k, q):
                n = f * G + k
                wait_pos(pool, sent[q], (f * (G // 2) + (k - q) // 2) * 16 * TPG)
                nc.gpsimd.tensor_copy(xn[:, q, :, C].bitcast(I32), numbers[:, bass.ds(k * TPG, TPG)]).then_inc(numbered, 1)
                pool.wait_ge(numbered, n + 1)
                pool.wait_ge(slotted, n + 1)
                stand(pool)
                for t in range(TPG):
                    nc.gpsimd.indirect_dma_start(
                        dispatched[:, :], bass.IndirectOffsetOnAxis(slot[:, q, t:t + 1], 0),
                        xn[:, q, t, :], None, bounds_check=last_row).then_inc(sent[q], 16)

            def front(f, k, ks):
                if f == 0 and valid(ks + 1) or f == 1 and valid(ks + 1):
                    rstd("f", f * G + k + 1, (ks + 1) % 2)
                if valid(ks):
                    scatter(f, k, ks % 2)

            def middle(k, ks):
                if valid(ks + 2):
                    rstd("a", k + 2, ks % 2)
                front(1, k, ks)

            def experts(f):
                def tokens(j, s):
                    pool.wait_ge(blk_in[s], (f * LOADS + j + 1) * 16)
                    wait_pos(pool, blk_out[s], (f * slot_blocks(s) + j) * 16)
                    nc.gpsimd.tensor_tensor(token[:, s:s + 1], xs[:, s, C:C + 1].bitcast(I32),
                                            to_replica[:, bass.ds(j * BU + s, 1)], ALU.add).then_inc(blk_tok, 1)

                def send(j, s):
                    pool.wait_ge(blk_tok, f * NB + j * BU + s + 1)
                    pool.wait_ge(blk_y, f * NB + j * BU + s + 1)
                    stand(pool)
                    nc.gpsimd.indirect_dma_start(
                        returned[:, :], bass.IndirectOffsetOnAxis(token[:, s:s + 1], 0),
                        ey[:, s, :], None, bounds_check=last_back).then_inc(blk_out[s], 16)

                def step(j, s, more=True):
                    if more:
                        tokens(j + (s + 1) // BU, (s + 1) % BU)
                    send(j, s)

                pool.wait_ge(table_ready, f + 1)
                tokens(0, 0)
                with_blocks(pool, step)

            pool.wait_ge(const_made, 4)
            rstd("f", 0, 0)
            nc.gpsimd.memset(xn[:, :, :, C + 1:ROW], 0.0).then_inc(const_made, 1)
            chain(nc.gpsimd.memset(ones[:], 1.0))
            nc.gpsimd.affine_select(out=before[:], in_=ones[:], compare_op=ALU.is_gt, fill=0.0, base=0,
                                    pattern=[[1, P]], channel_multiplier=-1).then_inc(const_made, 1)
            nc.gpsimd.iota(by_tile(region[:]), [[0, TPG], [CAP, E]], base=0, channel_multiplier=0,
                           **small).then_inc(const_made, 1)
            nc.gpsimd.iota(by_tile(prefer[:]), [[0, TPG], [-1, E]], base=E, channel_multiplier=0,
                           **small).then_inc(const_made, 1)
            nc.gpsimd.iota(numbers[:], [[P, NT]], base=0, channel_multiplier=1, **small).then_inc(const_made, 1)
            nc.gpsimd.iota(pad_base[:], [[CAP, E]], base=0, channel_multiplier=0, **small).then_inc(const_made, 1)
            nc.gpsimd.iota(block_no[:], [[1, NBL]], base=0, channel_multiplier=0, **small).then_inc(const_made, 1)
            nc.gpsimd.memset(blk_exp[:], 0.0).then_inc(const_made, 1)
            for u in range(BU):
                nc.gpsimd.memset(digit[:, u:u + 1], float(E ** u)).then_inc(const_made, 1)
            chain(nc.gpsimd.memset(upto[:], 1.0))
            nc.gpsimd.affine_select(out=upto[:], in_=upto[:], compare_op=ALU.is_ge, fill=0.0, base=0,
                                    pattern=[[1, E], [-1, E]], channel_multiplier=0).then_inc(const_made, 1)
            chain(nc.gpsimd.memset(pads[:], 0.0))
            nc.gpsimd.iota(pads[:, :, C:C + 1].bitcast(I32), [[P, E], [0, 1]], base=N, channel_multiplier=1,
                           **small).then_inc(const_made, 1)
            nc.gpsimd.memset(seen[:, 0, :], 0.0).then_inc(const_made, 1)

            pipeline(pool, lambda k, ks: front(0, k, ks), 0, G, 3, (G - 4) // 2, 2)
            experts(0)
            pipeline(pool, middle, -2, G, 1, (G - 4) // 2, 2)
            experts(1)

        @block.scalar
        def _(act):
            def norm(kind, n, k, q, dst):
                act.wait_ge(rstd_done[kind], n * RSTD_STEPS + RSTD_STEPS)
                stand(act)
                for t in range(TPG):
                    last = nc.scalar.activation(dst[:, q, t, 0:C], tile(xres, k * TPG + t), ACT.Identity,
                                                bias=shift[kind][:, q, t:t + 1], scale=scale[kind][:, q, t:t + 1])
                last.then_inc(normed[kind], 1)

            def norm_rows(f, k, ks):
                q = ks % 2
                wait_pos(act, sent[q], (f * (G // 2) + (k - q) // 2) * 16 * TPG)
                norm("f", f * G + k, k, q, xn)

            def front(f, k, ks):
                n = f * G + k
                if valid(ks):
                    act.wait_ge(turned["f"], n + 1)
                    wait_pos(act, gu_done, (n - 1) * HH)
                    nc.scalar.activation(xnT[:, ks % 2, :], tp["f"][:], ACT.Copy).then_inc(xnT_ready, 1)
                for h in range(HH):
                    if valid(ks - 1):
                        act.wait_ge(gu_done, (n - 1) * HH + h + 1)
                        wait_pos(act, mult_done, (n - 2) * HH + h + 1)
                        nc.scalar.activation(sg[:, h, :], g_ps[h][:], ACT.Silu).then_inc(silu_done, 1)

                if valid(ks + 1):
                    norm_rows(f, k + 1, ks + 1)

            def middle(k, ks):
                if valid(ks + 2):
                    wait_pos(act, x2_read, k + 1)
                    norm("a", k + 2, k + 2, ks % 2, xa)
                front(1, k, ks)

            def experts(f):
                def evac_pair(j, pair):
                    act.wait_ge(blk_turn, f * LOADS * PAIRS + j * PAIRS + pair + 1)
                    n = j * BU + pair * 2 - 2
                    wait_pos(act, blk_gu, f * NB if isinstance(n, int) and n < 2 else f * NB + n)
                    nc.scalar.activation(xsT[:, pair % 2, :, :],
                                         bank[pair % 2][:, 0:2 * P].rearrange("p (s c) -> p s c", s=2),
                                         ACT.Copy).then_inc(blk_xT, 1)

                def silu(b, r):
                    act.wait_ge(blk_gu, f * NB + b + 1)
                    wait_pos(act, blk_mul, f * NB + b - 1)
                    nc.scalar.activation(eg[:, r, :], bank[4 + r][:, 0:H], ACT.Silu).then_inc(blk_silu, 1)

                def evac_y(j, s):
                    act.wait_ge(blk_dn, f * NB + j * BU + s + 1)
                    wait_pos(act, blk_out[s], 16 * (f * slot_blocks(s) + j))
                    nc.scalar.activation(ey[:, s, :], bank[2 + s % 2][:, 0:C], ACT.Copy).then_inc(blk_y, 1)

                def step(j, s, more=True):
                    if more:
                        silu(j * BU + s + 1, (s + 1) % 2)
                    if not (isinstance(j, int) and j * BU + s == 0):
                        evac_y(j + (s - 1) // BU, (s - 1) % BU)
                    if s % 2 and ahead(j, s):
                        evac_pair(j + (s + 3) // BU, (s + 3) % BU // 2)

                evac_pair(0, 0)
                evac_pair(0, 1)
                silu(0, 0)
                with_blocks(act, step)
                evac_y((NB - 1) // BU, (NB - 1) % BU)

            pipeline(act, lambda k, ks: front(0, k, ks), -1, G, 3, (G - 4) // 2, 2)
            act.wait_ge(small_in, 16 * 5)
            nc.scalar.activation(decay[:, 1:2], decay[:, 0:1], ACT.Tanh, scale=0.5).then_inc(tanh_done, 1)
            experts(0)
            pipeline(act, middle, -2, G, 1, (G - 4) // 2, 2)
            experts(1)

        @block.vector
        def _(dve):
            def stats_of(kind, n, k, ks):
                wait_pos(dve, rstd_done[kind], (n - 1) * RSTD_STEPS)
                wait_pos(dve, stats[kind], n)
                stand(dve)
                for t in range(TPG):
                    last = nc.vector.bn_stats(st[kind][:, t, :], tile(xres, k * TPG + t))
                last.then_inc(bn_done[kind], 1)
                dve.wait_ge(bn_done[kind], n + 1)
                stand(dve)
                for t in range(TPG):
                    last = nc.vector.bn_aggr(mv[kind][:, ks % 2, t, :], st[kind][:, t, :])
                last.then_inc(stats[kind], 1)

            def add_back(k, q, done):
                nc.vector.scalar_tensor_tensor(out=tiles(xres, k), in0=back[:, q, :, :], scalar=0.5,
                                               in1=tiles(xres, k), op0=ALU.mult, op1=ALU.add).then_inc(done, 1)

            def scan(k, ks):
                dve.wait_ge(turned["a"], k + 1)
                wait_pos(dve, mixed, k - 1)
                nc.vector.tensor_tensor_scan(scanned[:, ks % 2, :], keep[:], tp["a"][:], 0.0, ALU.mult,
                                             ALU.add).then_inc(scan_done, 1)

            def add_attention(k, ks):
                dve.wait_ge(mixed, k + 1)
                nc.vector.tensor_tensor(attn_sum[:], xa[:, ks % 2, :, :].rearrange("p t c -> p (t c)"), o_ps[:],
                                        ALU.add).then_inc(x2_read, 1)
                dve.wait_ge(x2_read, k + 1)
                nc.vector.tensor_tensor(tiles(xres, k), tiles(xres, k), by_tile(attn_sum[:]),
                                        ALU.add).then_inc(x2_done, 1)
                dve.wait_ge(x2_done, k + 1)

            def mult(n, h):
                dve.wait_ge(silu_done, n * HH + h + 1)
                wait_pos(dve, down_done, n)
                nc.vector.tensor_tensor(hs[:, h, :], sg[:, h, :], u_ps[h][:], ALU.mult).then_inc(mult_done, 1)

            def add_shared(n, k):
                dve.wait_ge(down_done, n + 1)
                nc.vector.scalar_tensor_tensor(out=tiles(xres, k), in0=by_tile(o_ps[:]), scalar=0.5,
                                               in1=tiles(xres, k), op0=ALU.mult, op1=ALU.add).then_inc(half_done, 1)

            def choose(n, q):
                step = [0]

                def link(ins):
                    step[0] += 1
                    ins.then_inc(route, 1)
                    dve.wait_ge(route, n * ROUTE_STEPS + step[0])

                lg, pr, one = by_tile(rt[:, LOG]), by_tile(prefer[:]), chosen[:, q, :, :]
                dve.wait_ge(logits, n + 1)
                wait_pos(dve, route, n * ROUTE_STEPS)
                link(nc.vector.tensor_reduce(top[:], lg, AX.X, ALU.max))
                link(nc.vector.tensor_tensor(cand[:], lg, top[:].unsqueeze(2).to_broadcast([P, TPG, E]), ALU.is_ge))
                link(nc.vector.tensor_tensor(cand[:], cand[:], pr, ALU.mult))
                link(nc.vector.tensor_reduce(first[:], cand[:], AX.X, ALU.max))
                link(nc.vector.tensor_tensor(one, pr, first[:].unsqueeze(2).to_broadcast([P, TPG, E]), ALU.is_equal))
                link(nc.vector.tensor_reduce(seen_now[:], one.rearrange("p t e -> p e t"), AX.X, ALU.add))
                link(nc.vector.tensor_tensor(seen[:, 1 - q, :], seen[:, q, :], seen_now[:], ALU.add))

            def place_rows(f, n, k, q):
                dve.wait_ge(ranked, n + 1)
                wait_pos(dve, slotted, n)
                nc.vector.tensor_tensor(place[:], by_tile(rt[:, RANK]), by_tile(region[:]), ALU.add).then_inc(route, 1)
                dve.wait_ge(route, n * ROUTE_STEPS + 8)
                nc.vector.tensor_tensor(place[:], place[:], chosen[:, q, :, :], ALU.mult).then_inc(route, 1)
                dve.wait_ge(route, n * ROUTE_STEPS + 9)
                wait_pos(dve, sent[q], (f * (G // 2) + (k - q) // 2) * 16 * TPG)
                with nc.allow_low_precision("whole numbers"):
                    nc.vector.tensor_reduce(slot[:, q, :], place[:], AX.X, ALU.add).then_inc(slotted, 1)

            def front(f, k, ks):
                n = f * G + k
                if f == 0 and valid(ks + 1):
                    dve.wait_ge((x_in0, x_in1, x_rest)[min(ks + 1, 2)], 16)
                    stats_of("f", n + 1, k + 1, ks + 1)
                if valid(ks - 1):
                    mult(n - 1, 0)
                if valid(ks):
                    choose(n, ks % 2)
                if f == 1 and valid(ks + 1):
                    add_attention(k + 1, ks + 1)
                    stats_of("f", n + 1, k + 1, ks + 1)
                if valid(ks):
                    place_rows(f, n, k, ks % 2)
                if valid(ks - 1):
                    mult(n - 1, 1)
                if valid(ks - 1):
                    add_shared(n - 1, k - 1)

            def middle(k, ks):
                if valid(ks + 2):
                    dve.wait_ge(back_in[ks % 2], (k - ks % 2) // 2 * 16 + 32)
                    add_back(k + 2, ks % 2, x1_done)
                    dve.wait_ge(x1_done, k + 3)
                    stats_of("a", k + 2, k + 2, ks + 2)
                if valid(ks + 1):
                    scan(k + 1, ks + 1)
                front(1, k, ks)

            def tables(f):
                step = [0]

                def link(ins):
                    step[0] += 1
                    ins.then_inc(tabs, 1)
                    dve.wait_ge(tabs, f * TAB_STEPS + step[0])

                dve.wait_ge(totals, f + 1)
                wait_pos(dve, table_ready, f)
                tot = rt[:, TOT]
                nc.vector.tensor_tensor(pad_row[:], tot, pad_base[:], ALU.add).then_inc(pads_at, 1)
                link(nc.vector.tensor_scalar(n_up[:], tot, float(P - 1), None, ALU.add))
                link(nc.vector.tensor_scalar(n_blk[:], n_up[:], P.bit_length() - 1, None, ALU.logical_shift_right))
                link(nc.vector.tensor_copy(blk[:], n_blk[:]))
                link(nc.vector.tensor_tensor(blk_upto[:], upto[:], blk[:].unsqueeze(1).to_broadcast([P, E, E]),
                                             ALU.mult))
                link(nc.vector.tensor_reduce(blk_end[:], blk_upto[:], AX.X, ALU.add))
                link(nc.vector.tensor_scalar(last_blk[:], blk_end[:, E - 1:E], -1.0, None, ALU.add))
                link(nc.vector.tensor_scalar(real_blk[:], block_no[:], last_blk[:], None, ALU.min))
                link(nc.vector.tensor_tensor(past[:], real_blk[:].unsqueeze(2).to_broadcast([P, NBL, E]),
                                             blk_end[:].unsqueeze(1).to_broadcast([P, NBL, E]), ALU.is_ge))
                exps = blk_exp[:, 1:1 + NBL]
                link(nc.vector.tensor_reduce(exps, past[:], AX.X, ALU.add))
                link(nc.vector.tensor_tensor(past_n[:], past[:], blk[:].unsqueeze(1).to_broadcast([P, NBL, E]),
                                             ALU.mult))
                link(nc.vector.tensor_reduce(blk_from[:], past_n[:], AX.X, ALU.add))
                link(nc.vector.tensor_tensor(blk_from[:], real_blk[:], blk_from[:], ALU.subtract))
                link(nc.vector.tensor_scalar(blk_from[:], blk_from[:], float(P), None, ALU.mult))
                link(nc.vector.tensor_tensor(extra[:], block_no[:], real_blk[:], ALU.subtract))
                link(nc.vector.tensor_scalar(to_replica[:], extra[:], float(DUMP), None, ALU.mult))
                for u, at in (("up", 2), ("down", 0)):
                    link(nc.vector.tensor_tensor(packed[u][:], blk_exp[:, at:at + NBL].rearrange("p (j s) -> p j s", s=BU),
                                                 digit[:].unsqueeze(1).to_broadcast([P, LOADS, BU]), ALU.mult))
                    with nc.allow_low_precision("whole numbers below 2 ** 24"):
                        link(nc.vector.tensor_reduce(tab_exp[u][:], packed[u][:], AX.X, ALU.add))
                nc.vector.scalar_tensor_tensor(out=tab_row[:], in0=exps, scalar=float(CAP), in1=blk_from[:],
                                               op0=ALU.mult, op1=ALU.add).then_inc(table_ready, 1)

            def experts(f):
                def mul(b, r):
                    dve.wait_ge(blk_silu, f * NB + b + 1)
                    wait_pos(dve, blk_hturn, f * NB + b - 1)
                    nc.vector.tensor_tensor(eh[:, r, :], eg[:, r, :], bank[4 + r][:, H:2 * H],
                                            ALU.mult).then_inc(blk_mul, 1)

                def evac_h(b, r):
                    dve.wait_ge(blk_hturn, f * NB + b + 1)
                    wait_pos(dve, blk_dn, f * NB + b - 1)
                    nc.vector.tensor_copy(ehT[:, r, :], bank[6 + r][:, 0:H]).then_inc(blk_hT, 1)

                def step(j, s, more=True):
                    if more:
                        mul(j * BU + s + 1, (s + 1) % 2)
                    evac_h(j * BU + s, s % 2)

                mul(0, 0)
                with_blocks(dve, step)

            pipeline(dve, lambda k, ks: front(0, k, ks), -1, G, 3, (G - 4) // 2, 2)
            dve.wait_ge(mix_raw, 1)
            nc.vector.tensor_scalar(mix[:], tp["a"][:, 0:C], gate[:], None, ALU.mult).then_inc(setup, 1)
            tables(0)
            dve.wait_ge(tanh_done, 1)
            nc.vector.tensor_scalar(decay[:, 0:1], decay[:, 1:2], 0.5, 0.5, ALU.mult, ALU.add).then_inc(setup, 1)
            nc.vector.memset(keep[:], 1.0).then_inc(setup, 1)
            nc.vector.memset(seen[:, 0, :], 0.0).then_inc(setup, 1)
            dve.wait_ge(setup, 4)
            nc.vector.tensor_scalar(keep[:], keep[:], decay[:, 0:1], None, ALU.mult).then_inc(setup, 1)
            dve.wait_ge(setup, 5)
            nc.vector.memset(keep[:].rearrange("p (b t) -> p b t", t=T)[:, :, 0], 0.0).then_inc(setup, 1)
            dve.wait_ge(setup, 6)
            experts(0)
            dve.wait_ge(half_done, G)
            pipeline(dve, middle, -2, G, 1, (G - 4) // 2, 2)
            tables(1)
            experts(1)
            dve.wait_ge(half_done, 2 * G)
            for k in range(G):
                dve.wait_ge(back_in[k % 2], (G // 2 + k // 2 + 1) * 16)
                add_back(k, k % 2, x3_done)

        @block.tensor
        def _(pe):
            def turn(kind, n, q, src, free):
                pe.wait_ge(normed[kind], n + 1)
                wait_pos(pe, free, n)
                for t in range(TPG):
                    last = nc.tensor.transpose(tp[kind][:, t * P:(t + 1) * P], src[:, q, t, 0:C], ident[:])
                last.then_inc(turned[kind], 1)

            def gate_up(n, q, h):
                pe.wait_ge(xnT_ready, n + 1)
                wait_pos(pe, mult_done, (n - 1) * HH + h + 1)
                for ps, at in ((g_ps[h], h * P), (u_ps[h], H + h * P)):
                    last = nc.tensor.matmul(ps[:], gu[:, SHARED, at:at + P], xnT[:, q, :], start=True, stop=True)
                last.then_inc(gu_done, 1)

            def down(n):
                pe.wait_ge(mult_done, (n + 1) * HH)
                for t in range(TPG):
                    for h in range(HH):
                        last = nc.tensor.matmul(o_ps[:, t * C:(t + 1) * C], hs[:, h, t * P:(t + 1) * P],
                                                dn[:, SHARED, h, :], start=(h == 0), stop=(h == HH - 1))
                last.then_inc(down_done, 1)

            def front(f, k, ks):
                n, q = f * G + k, ks % 2
                if valid(ks):
                    turn("f", n, q, xn, xnT_ready)
                if f == 1 and valid(ks + 1):
                    turn("a", k + 1, 1 - q, xa, scan_done)
                if valid(ks - 1):
                    gate_up(n - 1, 1 - q, 0)
                if valid(ks):
                    pe.wait_ge(xnT_ready, n + 1)
                    wait_pos(pe, route, (n - 1) * ROUTE_STEPS + 8)
                    for t in range(TPG):
                        last = nc.tensor.matmul(rt[:, t * E:(t + 1) * E], xnT[:, q, t * P:(t + 1) * P], routerT[:],
                                                start=True, stop=True)
                    last.then_inc(logits, 1)
                if f == 1 and valid(ks + 1):
                    pe.wait_ge(scan_done, k + 2)
                    if ks - 2 >= 0:
                        pe.wait_ge(half_done, G + k - 1)
                    for t in range(TPG):
                        last = nc.tensor.matmul(o_ps[:, t * C:(t + 1) * C], scanned[:, 1 - q, t * P:(t + 1) * P],
                                                mix[:], start=True, stop=True)
                    last.then_inc(mixed, 1)
                if valid(ks - 1):
                    gate_up(n - 1, 1 - q, 1)
                if valid(ks):
                    pe.wait_ge(route, n * ROUTE_STEPS + 7)
                    one, ranks = chosen[:, q, :, :], by_tile(rt[:, RANK])
                    nc.tensor.matmul(ranks, before[:], one, start=True, stop=False)
                    for t in range(TPG - 1):
                        nc.tensor.matmul(ranks[:, t + 1:TPG, :], ones[:],
                                         one[:, t:t + 1, :].to_broadcast([P, TPG - 1 - t, E]), start=False, stop=False)
                    nc.tensor.matmul(ranks, ones[:], seen[:, q, :].unsqueeze(1).to_broadcast([P, TPG, E]),
                                     start=False, stop=True).then_inc(ranked, 1)
                if valid(ks - 1):
                    if f == 1 and valid(ks + 1):
                        pe.wait_ge(x2_read, k + 2)
                    else:
                        wait_pos(pe, half_done, n - 1)
                    down(n - 1)

            def count_all(f):
                pe.wait_ge(route, ((f + 1) * G - 1) * ROUTE_STEPS + 8)
                nc.tensor.matmul(rt[:, TOT], ones[:], seen[:, G % 2, :], start=True, stop=True).then_inc(totals, 1)

            def experts(f):
                def turn_pair(j, pair):
                    n = f * LOADS * PAIRS + j * PAIRS + pair
                    wait_pos(pe, blk_xT, n - 1)
                    for s in (2 * pair, 2 * pair + 1):
                        pe.wait_ge(blk_in[s], (f * LOADS + j + 1) * 16)
                        last = nc.tensor.transpose(bank[pair % 2][:, s % 2 * P:(s % 2 + 1) * P], xs[:, s, 0:C],
                                                   ident[:])
                    last.then_inc(blk_turn, 1)

                def gate_up_block(j, s, e):
                    b = j * BU + s
                    pe.wait_ge(blk_xT, f * LOADS * PAIRS + j * PAIRS + s // 2 + 1)
                    wait_pos(pe, blk_mul, f * NB + b - 1)
                    nc.tensor.matmul(bank[4 + s % 2][:], xsT[:, s // 2 % 2, s % 2, :], tile(gu, e), start=True,
                                     stop=True).then_inc(blk_gu, 1)

                def turn_hidden(b, r):
                    pe.wait_ge(blk_mul, f * NB + b + 1)
                    wait_pos(pe, blk_hT, f * NB + b - 1)
                    for h in range(HH):
                        last = nc.tensor.transpose(bank[6 + r][:, h * P:(h + 1) * P], eh[:, r, h * P:(h + 1) * P],
                                                   ident[:])
                    last.then_inc(blk_hturn, 1)

                def down_block(j, s, e):
                    b = j * BU + s
                    pe.wait_ge(blk_hT, f * NB + b + 1)
                    wait_pos(pe, blk_y, f * NB + b - 1)
                    for h in range(HH):
                        last = nc.tensor.matmul(bank[2 + s % 2][:, 0:C], ehT[:, s % 2, h * P:(h + 1) * P],
                                                dn[:, bass.ds(e, 1), h, :].rearrange("p a c -> p (a c)"),
                                                start=(h == 0), stop=(h == HH - 1))
                    last.then_inc(blk_dn, 1)

                exps = {}

                def step(j, s, more=True):
                    if s == 0:
                        for u in ("up", "down"):
                            exps[u] = pe.value_load(tab_exp[u][0:1, bass.ds(j, 1)], min_val=0, max_val=E ** BU - 1)
                    if more:
                        gate_up_block(j + (s + 1) // BU, (s + 1) % BU, (exps["up"] >> 3 * s) & E - 1)
                    turn_hidden(j * BU + s, s % 2)
                    if not (isinstance(j, int) and j * BU + s == 0):
                        down_block(j + (s - 1) // BU, (s - 1) % BU, (exps["down"] >> 3 * s) & E - 1)
                    if s % 2 and ahead(j, s):
                        turn_pair(j + (s + 3) // BU, (s + 3) % BU // 2)

                pe.wait_ge(table_ready, f + 1)
                turn_pair(0, 0)
                turn_pair(0, 1)
                first = pe.value_load(tab_exp["down"][0:1, 0:1], min_val=0, max_val=E ** BU - 1)
                gate_up_block(0, 0, (first >> 3) & E - 1)
                with_blocks(pe, step)
                down_block((NB - 1) // BU, (NB - 1) % BU, (exps["down"] >> 3 * (NB % BU)) & E - 1)

            pe.wait_ge(const_made, N_CONST)
            pe.wait_ge(small_in, 16 * 5)
            nc.tensor.matmul(tp["a"][:, 0:C], hank_u[:], hank_b[:], start=True, stop=True).then_inc(mix_raw, 1)
            pe.wait_ge(shared_in, 16 * 2)
            pipeline(pe, lambda k, ks: front(0, k, ks), 0, G, 3, (G - 4) // 2, 2)
            count_all(0)
            pe.wait_ge(experts_in, 16 * 2)
            pe.wait_ge(setup, 1)
            experts(0)
            pe.wait_ge(setup, 6)
            pipeline(pe, lambda k, ks: front(1, k, ks), -1, G, 1, (G - 4) // 2, 2)
            count_all(1)
            experts(1)


def kernel(L0_attn_x, L0_attn_bind_key, L0_attn_unbind_key, L0_attn_gate, L0_attn_decay, L0_ffn_up, L0_ffn_gate,
           L0_ffn_down, L0_ffn_router, L0_ffn_w_up_s, L0_ffn_w_gate_s, L0_ffn_w_down_s):
    import numpy as np
    import concourse.bacc as bacc
    from concourse.bass_utils import run_bass_kernel_spmd

    def a(x):
        return np.asarray(x)

    gates = np.concatenate([a(L0_ffn_gate), a(L0_ffn_w_gate_s)[None]], 0)
    ups = np.concatenate([a(L0_ffn_up), a(L0_ffn_w_up_s)[None]], 0)
    gu = np.concatenate([gates, ups], 1).transpose(2, 0, 1)
    downs = np.concatenate([a(L0_ffn_down), a(L0_ffn_w_down_s)[None]], 0)
    dn = downs.reshape(E + 1, C, HH, P).transpose(3, 0, 2, 1)
    arrays = {
        "x": a(L0_attn_x),
        "gu": gu,
        "dn": dn,
        "router": a(L0_ffn_router).T,
        "bind": np.concatenate([a(L0_attn_bind_key)] * 2),
        "unbind": np.concatenate([a(L0_attn_unbind_key)] * 2),
        "gate": a(L0_attn_gate).reshape(1),
        "decay": a(L0_attn_decay).reshape(1),
    }
    arrays = {name: np.ascontiguousarray(v) for name, v in arrays.items()}
    nc = bacc.Bacc("TRN2", target_bir_lowering=False, num_devices=1)
    ins = [nc.dram_tensor("in_" + name, v.shape, mybir.dt.from_np(v.dtype), kind="ExternalInput").ap()
           for name, v in arrays.items()]
    out = nc.dram_tensor("out", (B, T, C), F32, kind="ExternalOutput").ap()
    build(nc, *ins, out)
    r = run_bass_kernel_spmd(nc, [{"in_" + name: v for name, v in arrays.items()}], core_ids=[0])
    return r.results[0]["out"]
```

```python
from contextlib import ExitStack

import concourse.bass as bass
from concourse import mybir

ALU = mybir.AluOpType
ACT = mybir.ActivationFunctionType
AX = mybir.AxisListType
F32 = mybir.dt.float32
BF16 = mybir.dt.bfloat16
I32 = mybir.dt.int32

P = 128
C = 128
E = 8
SHARED = E
H = 256
HH = H // P
B, T = 16, 256
N = B * T
NT = N // P
TPG = 4
G = NT // TPG
GC = TPG * P
ROW = C + 4
CAP = N + P
X_LOADS = ((0, 1), (1, 2), (2, 4), (4, G))
NB = NT + E - 1
NBL = NB + 1
PADS_SP = 6
WR = 4
FETCH = 3
BU = 8
PAIRS = BU // 2
DUMP = N + E * P
EPS = 1e-05


LOADS = NBL // BU
ROUTE_STEPS = 7
RSTD_STEPS = 4
TAB_STEPS = 17
N_CONST = 10
N_TABLE_CONST = 5 + BU


def slot_blocks(s):
    return len(range(s, NB, BU))


def ahead(j, s):
    return not isinstance(j, int) or j * BU + s + 3 < NBL


def with_blocks(eng, step):
    for s in range(BU):
        step(0, s)
    with eng.Fori(1, NB // BU) as j:
        for s in range(BU):
            step(j, s)
    for b in range(NB // BU * BU, NB):
        step(b // BU, b % BU, more=b + 1 < NB)


def build(nc, x_in, gu_in, dn_in, router_in, bind_in, unbind_in, gate_in, decay_in, out):
    x_dram = x_in.rearrange("b t c -> (b t) c").rearrange("(i p) c -> p i c", p=P)
    out_dram = out.rearrange("b t c -> (b t) c").rearrange("(i p) c -> p i c", p=P)
    dispatched = nc.dram_tensor("dispatched", [E * CAP, ROW], F32, kind="Internal")
    returned = nc.dram_tensor("returned", [DUMP * (E + 1), C], F32, kind="Internal")
    returned_tiles = returned[0:N, :].rearrange("(i p) c -> p i c", p=P)

    with ExitStack() as ctx:
        def sb(name, shape, dt=F32):
            return ctx.enter_context(nc.sbuf_tensor(name, shape, dt))

        def sem(name):
            return ctx.enter_context(nc.semaphore(name))

        gu = sb("gu", [P, E + 1, 2 * H])
        dn = sb("dn", [P, E + 1, HH, C])
        routerT = sb("routerT", [P, E])
        ident = sb("ident", [P, P])
        before = sb("before", [P, P], BF16)
        ones = sb("ones", [P, P], BF16)
        region = sb("region", [P, E], BF16)
        prefer = sb("prefer", [P, TPG * E])
        pad_base = sb("pad_base", [P, E])
        upto = sb("upto", [P, E, E])
        block_no = sb("block_no", [P, NBL])
        minus_half = sb("minus_half", [P, TPG])
        minus_one = sb("minus_one", [P, TPG])
        eps = sb("eps", [P, TPG])
        pads = sb("pads", [P, E, ROW])
        hank_b = sb("hank_b", [P, P])
        hank_u = sb("hank_u", [P, P])
        mix = sb("mix", [P, C])
        gate = sb("gate", [P, 1])
        decay = sb("decay", [P, 2])
        keep = sb("keep", [P, GC])

        xres = sb("xres", [P, NT, C])
        xn = sb("xn", [P, NT, ROW])
        xa = sb("xa", [P, 2 * TPG, C])
        back = sb("back", [P, NT, C])
        xnT = sb("xnT", [P, 2, GC])
        scanned = sb("scanned", [P, 2, GC])
        st = {k: sb("st_" + k, [P, TPG, 6]) for k in "fa"}
        mv = {k: sb("mv_" + k, [P, NT, 2]) for k in "fa"}
        var = {k: sb("var_" + k, [P, TPG]) for k in "fa"}
        mr = {k: sb("mr_" + k, [P, TPG]) for k in "fa"}
        scale = {k: sb("scale_" + k, [P, NT]) for k in "fa"}
        shift = {k: sb("shift_" + k, [P, NT]) for k in "fa"}
        scale_more = sb("scale_more", [P, NT])

        top = sb("top", [P, TPG])
        cand = sb("cand", [P, TPG, E])
        first = sb("first", [P, TPG])
        chosen = sb("chosen", [P, 2, TPG + 1, E], BF16)
        place = sb("place", [P, TPG, E])
        slot = sb("slot", [P, NT], I32)
        pad_row = sb("pad_row", [P, E], I32)
        n_up = sb("n_up", [P, E], I32)
        n_blk = sb("n_blk", [P, E], I32)
        blk = sb("blk", [P, E])
        blk_upto = sb("blk_upto", [P, E, E])
        blk_end = sb("blk_end", [P, E])
        last_blk = sb("last_blk", [P, 1])
        real_blk = sb("real_blk", [P, NBL])
        past = sb("past", [P, NBL, E])
        past_n = sb("past_n", [P, NBL, E])
        blk_exp = sb("blk_exp", [P, (LOADS + 1) * BU])
        blk_from = sb("blk_from", [P, NBL])
        extra = sb("extra", [P, NBL])
        to_replica = sb("to_replica", [P, NBL], I32)
        digit = sb("digit", [P, BU])
        packed = sb("packed", [P, LOADS + 1, BU])
        tab_exp = sb("tab_exp", [P, LOADS + 1], I32)
        tab_row = sb("tab_row", [P, NBL], I32)

        sg = sb("sg", [P, HH, GC])
        hs = sb("hs", [P, 2, HH, GC])

        xs = sb("xs", [P, BU, ROW])
        token = sb("token", [P, BU], I32)
        xsT = sb("xsT", [P, 2, 2, P])
        eg = sb("eg", [P, 2, H])
        eh = sb("eh", [P, 2, H])
        wgu = sb("wgu", [P, WR, 2 * H])
        wdn = sb("wdn", [P, WR, HH * C])
        ey = sb("ey", [P, BU, C])

        bank = [ctx.enter_context(nc.psum_tensor(f"bank{i}", [P, GC], F32)) for i in range(8)]
        tp = {"f": bank[0], "a": bank[1]}
        rt = bank[2]
        o_ps = bank[3]
        g_ps, u_ps = [bank[4], bank[6]], [bank[5], bank[7]]
        LOG, RANK, TOT = slice(0, 32), slice(32, 64), slice(64, 64 + E)

        const_made = sem("const_made")
        table_const = sem("table_const")
        const_chain = sem("const_chain")
        x_in = [sem(f"x_in{i}") for i in range(len(X_LOADS))]
        small_in = sem("small_in")
        shared_in, experts_in = sem("shared_in"), sem("experts_in")
        tanh_done, setup, mix_raw = sem("tanh_done"), sem("setup"), sem("mix_raw")
        bn_done = {k: sem("bn_done_" + k) for k in "fa"}
        stats = {k: sem("stats_" + k) for k in "fa"}
        rstd_done = {k: sem("rstd_done_" + k) for k in "fa"}
        normed = {k: sem("normed_" + k) for k in "fa"}
        turned = {k: sem("turned_" + k) for k in "fa"}
        xnT_ready = sem("xnT_ready")
        logits = sem("logits")
        route = sem("route")
        ranked = sem("ranked")
        slotted = sem("slotted")
        sent = sem("sent")
        gu_done = sem("gu_done")
        silu_done, mult_done = sem("silu_done"), sem("mult_done")
        down_done, half_done = sem("down_done"), sem("half_done")
        totals, tabs, pads_at = sem("totals"), sem("tabs"), sem("pads_at")
        table_ready, pad_sent = sem("table_ready"), sem("pad_sent")
        back_in = [sem(f"back_in{k}") for k in range(G)]
        x1_done, scan_done, mixed = sem("x1_done"), sem("scan_done"), sem("mixed")
        selfed, x2_done = sem("selfed"), sem("x2_done")
        blk_in = [sem(f"blk_in{s}") for s in range(BU)]
        blk_out = [sem(f"blk_out{s}") for s in range(BU)]
        blk_tok = sem("blk_tok")
        blk_turn, blk_xT = sem("blk_turn"), sem("blk_xT")
        blk_wgu, blk_wdn = sem("blk_wgu"), sem("blk_wdn")
        blk_gu, blk_silu, blk_mul = sem("blk_gu"), sem("blk_silu"), sem("blk_mul")
        blk_dn, blk_y = sem("blk_dn"), sem("blk_y")
        x3_done, stored = sem("x3_done"), sem("stored")

        block = ctx.enter_context(nc.Block())

        def tiles(buf, k):
            return buf[:, k * TPG:(k + 1) * TPG, :]

        def cols(buf, k):
            return buf[:, k * TPG:(k + 1) * TPG]

        def tile(buf, i):
            return buf[:, bass.ds(i, 1), :].rearrange("p a c -> p (a c)")

        def by_tile(ap):
            return ap.rearrange("p (t e) -> p t e", t=TPG)

        def valid(k):
            return 0 <= k < G

        def is_int(j):
            return isinstance(j, int)

        def steps(body, lag, ahead):
            for k in range(-ahead, G + lag):
                body(k)

        def expert_of(digits, b):
            return digits >> 3 * ((b - FETCH) % BU) & E - 1

        def load_digits(eng, i):
            return eng.value_load(tab_exp[0:1, bass.ds(i, 1)], min_val=0, max_val=E ** BU - 1)

        def send_pads(eng, experts):
            for e in experts:
                row = eng.value_load(pad_row[0:1, e:e + 1], min_val=0, max_val=E * CAP - P)
                eng.dma_start(dispatched[bass.ds(row, P), :], pads[:, e, :]).then_inc(pad_sent, 16)

        def stand(eng):
            eng.nop(nofuse=True)

        def wait_pos(eng, s, value):
            if not (isinstance(value, int) and value <= 0):
                eng.wait_ge(s, value)

        @block.sync
        def _(sp):
            def load_x(i):
                lo, hi = X_LOADS[i]
                sp.dma_start(xres[:, lo * TPG:hi * TPG, :], x_dram[:, lo * TPG:hi * TPG, :]).then_inc(x_in[i], 16)

            load_x(0)
            load_x(1)
            sp.dma_start(routerT[:], router_in).then_inc(small_in, 16)
            sp.dma_start(gu[:, SHARED, :], gu_in[:, SHARED, :]).then_inc(shared_in, 16)
            sp.dma_start(dn[:, SHARED, :, :], dn_in[:, SHARED, :, :]).then_inc(shared_in, 16)
            load_x(2)
            for key, hank in ((bind_in, hank_b), (unbind_in, hank_u)):
                windows = bass.AP(key.tensor, 0, [[1, P], [1, P]])
                sp.dma_start(hank[:], windows).then_inc(small_in, 16)
            sp.dma_start(gate[:], gate_in.partition_broadcast(P)).then_inc(small_in, 16)
            sp.dma_start(decay[:, 0:1], decay_in.partition_broadcast(P)).then_inc(small_in, 16)
            load_x(3)
            sp.dma_start(gu[:, 0:E, :], gu_in[:, 0:E, :]).then_inc(experts_in, 16)
            sp.dma_start(dn[:, 0:E, :, :], dn_in[:, 0:E, :, :]).then_inc(experts_in, 16)

            def load_block(f, j, s):
                b = j * BU + s
                wait_pos(sp, blk_turn, f * (NBL // 2) + (j - 1) * PAIRS + s // 2 + 1)
                stand(sp)
                first_use = isinstance(j, int) and j == 0
                wait_pos(sp, blk_tok, f * NB if first_use else f * NB + b - BU + 1)
                stand(sp)
                row = sp.value_load(tab_row[0:1, bass.ds(b, 1)], min_val=0, max_val=E * CAP - P)
                sp.dma_start(xs[:, s, :], dispatched[bass.ds(row, P), :]).then_inc(blk_in[s], 16)

            sp.wait_ge(table_const, N_TABLE_CONST)
            for f in range(2):
                sp.wait_ge(pads_at, f + 1)
                send_pads(sp, range(0, PADS_SP))
                sp.wait_ge(table_ready, f + 1)
                sp.wait_ge(pad_sent, 16 * E * (f + 1))
                sp.wait_ge(sent, 16 * NT * (f + 1))
                for s in range(BU):
                    load_block(f, 0, s)
                with sp.Fori(1, LOADS) as j:
                    for s in range(BU):
                        load_block(f, j, s)
                for s in range(BU):
                    sp.wait_ge(blk_out[s], 16 * slot_blocks(s) * (f + 1))
                for k in range(G):
                    sp.dma_start(tiles(back, k), returned_tiles[:, k * TPG:(k + 1) * TPG, :]).then_inc(back_in[k], 16)
            sp.wait_ge(stored, 16 * G)

        @block.gpsimd
        def _(pool):
            chained = [0]
            small = dict(allow_small_or_imprecise_dtypes=True)

            def chain(ins):
                chained[0] += 1
                ins.then_inc(const_chain, 1)
                pool.wait_ge(const_chain, chained[0])

            chain(nc.gpsimd.memset(ident[:], 0.0))
            nc.gpsimd.affine_select(out=ident[:], in_=ident[:], compare_op=ALU.not_equal, fill=1.0, base=0,
                                    pattern=[[-1, P]], channel_multiplier=1).then_inc(const_made, 1)
            nc.gpsimd.memset(minus_half[:], -0.5).then_inc(const_made, 1)
            nc.gpsimd.memset(minus_one[:], -1.0).then_inc(const_made, 1)
            nc.gpsimd.memset(eps[:], EPS).then_inc(const_made, 1)
            nc.gpsimd.iota(xn[:, :, C:C + 1].bitcast(I32), [[P, NT], [0, 1]], base=0, channel_multiplier=1,
                           **small).then_inc(const_made, 1)
            last_row = pool.to_reg(E * CAP - 1)
            last_back = pool.to_reg(DUMP * (E + 1) - 1)

            def rstd(kind, n, k):
                s = rstd_done[kind]
                pool.wait_ge(stats[kind], n + 1)
                m, sc = tiles(mv[kind], k), cols(scale[kind], k)
                nc.gpsimd.tensor_tensor(var[kind][:], m[:, :, 1], eps[:], ALU.add).then_inc(s, 1)
                pool.wait_ge(s, n * RSTD_STEPS + 1)
                nc.gpsimd.tensor_tensor(sc, var[kind][:], minus_half[:], ALU.pow).then_inc(s, 1)
                pool.wait_ge(s, n * RSTD_STEPS + 2)
                nc.gpsimd.tensor_tensor(mr[kind][:], sc, m[:, :, 0], ALU.mult).then_inc(s, 1)
                if kind == "a":
                    nc.gpsimd.tensor_tensor(cols(scale_more, k), sc, minus_one[:], ALU.subtract)
                pool.wait_ge(s, n * RSTD_STEPS + 3)
                nc.gpsimd.tensor_tensor(cols(shift[kind], k), mr[kind][:], minus_one[:], ALU.mult).then_inc(s, 1)

            def scatter(f, k):
                pool.wait_ge(slotted, f * G + k + 1)
                for i in range(k * TPG, (k + 1) * TPG):
                    nc.gpsimd.indirect_dma_start(
                        dispatched[:, :], bass.IndirectOffsetOnAxis(slot[:, i:i + 1], 0),
                        xn[:, i, :], None, bounds_check=last_row).then_inc(sent, 16)

            def first_ffn(k):
                if valid(k + 2):
                    rstd("f", k + 2, k + 2)
                if valid(k):
                    scatter(0, k)

            def middle(k):
                if valid(k + 3):
                    rstd("a", k + 3, k + 3)
                if valid(k + 2):
                    rstd("f", G + k + 2, k + 2)
                if valid(k):
                    scatter(1, k)

            def experts(f):
                def tokens(j, s):
                    pool.wait_ge(blk_in[s], (f * LOADS + j + 1) * 16)
                    wait_pos(pool, blk_out[s], (f * slot_blocks(s) + j) * 16)
                    nc.gpsimd.tensor_tensor(token[:, s:s + 1], xs[:, s, C:C + 1].bitcast(I32),
                                            to_replica[:, bass.ds(j * BU + s, 1)], ALU.add).then_inc(blk_tok, 1)

                def send(j, s):
                    pool.wait_ge(blk_tok, f * NB + j * BU + s + 1)
                    pool.wait_ge(blk_y, f * NB + j * BU + s + 1)
                    stand(pool)
                    nc.gpsimd.indirect_dma_start(
                        returned[:, :], bass.IndirectOffsetOnAxis(token[:, s:s + 1], 0),
                        ey[:, s, :], None, bounds_check=last_back).then_inc(blk_out[s], 16)

                def step(j, s, more=True):
                    if more:
                        tokens(j + (s + 1) // BU, (s + 1) % BU)
                    send(j, s)

                pool.wait_ge(table_ready, f + 1)
                tokens(0, 0)
                with_blocks(pool, step)

            pool.wait_ge(const_made, 4)
            first_ffn(-2)
            nc.gpsimd.memset(xn[:, :, C + 1:ROW], 0.0).then_inc(const_made, 1)
            chain(nc.gpsimd.memset(ones[:], 1.0))
            nc.gpsimd.affine_select(out=before[:], in_=ones[:], compare_op=ALU.is_gt, fill=0.0, base=0,
                                    pattern=[[1, P]], channel_multiplier=-1).then_inc(const_made, 1)
            nc.gpsimd.iota(by_tile(prefer[:]), [[0, TPG], [-1, E]], base=E, channel_multiplier=0,
                           **small).then_inc(const_made, 1)
            nc.gpsimd.iota(region[:], [[CAP // P, E]], base=0, channel_multiplier=0, **small).then_inc(const_made, 1)
            nc.gpsimd.memset(chosen[:, 0, TPG, :], 0.0).then_inc(const_made, 1)
            first_ffn(-1)
            first_ffn(0)
            nc.gpsimd.iota(pad_base[:], [[CAP, E]], base=0, channel_multiplier=0, **small).then_inc(table_const, 1)
            nc.gpsimd.iota(block_no[:], [[1, NBL]], base=0, channel_multiplier=0, **small).then_inc(table_const, 1)
            nc.gpsimd.memset(blk_exp[:], 0.0).then_inc(table_const, 1)
            for u in range(BU):
                nc.gpsimd.memset(digit[:, u:u + 1], float(E ** u)).then_inc(table_const, 1)
            chain(nc.gpsimd.memset(upto[:], 1.0))
            nc.gpsimd.affine_select(out=upto[:], in_=upto[:], compare_op=ALU.is_ge, fill=0.0, base=0,
                                    pattern=[[1, E], [-1, E]], channel_multiplier=0).then_inc(table_const, 1)
            chain(nc.gpsimd.memset(pads[:], 0.0))
            nc.gpsimd.iota(pads[:, :, C:C + 1].bitcast(I32), [[P, E], [0, 1]], base=N, channel_multiplier=1,
                           **small).then_inc(table_const, 1)
            for k in range(1, G):
                first_ffn(k)
            experts(0)
            steps(middle, 0, 3)
            experts(1)

        @block.scalar
        def _(act):
            def norm(kind, n, k, dst, at):
                act.wait_ge(rstd_done[kind], (n + 1) * RSTD_STEPS)
                for t in range(TPG):
                    i = k * TPG + t
                    last = nc.scalar.activation(dst[:, at * TPG + t, 0:C], xres[:, i, :], ACT.Identity,
                                                bias=shift[kind][:, i:i + 1], scale=scale[kind][:, i:i + 1])
                last.then_inc(normed[kind], 1)

            def add_self(k):
                act.wait_ge(normed["a"], k + 1)
                for i in range(k * TPG, (k + 1) * TPG):
                    last = nc.scalar.activation(xres[:, i, :], xres[:, i, :], ACT.Identity,
                                                bias=shift["a"][:, i:i + 1], scale=scale_more[:, i:i + 1])
                last.then_inc(selfed, 1)

            def evac_rows(n):
                act.wait_ge(turned["f"], n + 1)
                wait_pos(act, gu_done, (n - 1) * HH)
                nc.scalar.activation(xnT[:, n % 2, :], tp["f"][:], ACT.Copy).then_inc(xnT_ready, 1)

            def silu_half(n, h):
                act.wait_ge(gu_done, n * HH + h + 1)
                wait_pos(act, mult_done, (n - 1) * HH + h + 1)
                nc.scalar.activation(sg[:, h, :], g_ps[h][:], ACT.Silu).then_inc(silu_done, 1)

            def front(f, k):
                n = f * G + k
                if valid(k):
                    evac_rows(n)
                if f == 1 and valid(k + 2):
                    add_self(k + 2)
                if valid(k + 1):
                    norm("f", n + 1, k + 1, xn, k + 1)
                for h in range(HH):
                    if valid(k - 1):
                        silu_half(n - 1, h)
                if k == G - 1:
                    act.wait_ge(pads_at, f + 1)
                    send_pads(act, range(PADS_SP, E))

            def middle(k):
                front(1, k)
                if valid(k + 3):
                    wait_pos(act, turned["a"], k + 2)
                    norm("a", k + 3, k + 3, xa, (k + 3) % 2)

            def experts(f):
                def evac_pair(j, pair):
                    act.wait_ge(blk_turn, f * LOADS * PAIRS + j * PAIRS + pair + 1)
                    n = j * BU + pair * 2 - 2
                    wait_pos(act, blk_gu, f * NB if isinstance(n, int) and n < 2 else f * NB + n)
                    nc.scalar.activation(xsT[:, pair % 2, :, :],
                                         bank[pair % 2][:, 0:2 * P].rearrange("p (s c) -> p s c", s=2),
                                         ACT.Copy).then_inc(blk_xT, 1)

                def silu(b, r):
                    act.wait_ge(blk_gu, f * NB + b + 1)
                    wait_pos(act, blk_mul, f * NB + b - 1)
                    nc.scalar.activation(eg[:, r, :], bank[4 + r][:, 0:H], ACT.Silu).then_inc(blk_silu, 1)

                def evac_y(j, s):
                    act.wait_ge(blk_dn, f * NB + j * BU + s + 1)
                    wait_pos(act, blk_out[s], 16 * (f * slot_blocks(s) + j))
                    nc.scalar.activation(ey[:, s, :], bank[2 + s % 2][:, 0:C], ACT.Copy).then_inc(blk_y, 1)

                def copy_down(b, r, e):
                    wait_pos(act, blk_dn, f * NB + b - WR + 1)
                    stand(act)
                    nc.scalar.activation(wdn[:, r, :], tile(dn[:].rearrange("p e h c -> p e (h c)"), e),
                                         ACT.Copy).then_inc(blk_wdn, 1)

                def step(j, s, more=True):
                    b = j * BU + s
                    if s == 0:
                        digits[0] = load_digits(act, j + 1)
                    if more:
                        silu(b + 1, (s + 1) % 2)
                    if is_int(j) and b == 0:
                        evac_pair(0, 1)
                    else:
                        evac_y(j + (s - 1) // BU, (s - 1) % BU)
                    if not is_int(j) or b + FETCH < NB:
                        copy_down(b + FETCH, (s + FETCH) % WR, expert_of(digits[0], s + FETCH))
                    if s % 2 and ahead(j, s):
                        evac_pair(j + (s + 3) // BU, (s + 3) % BU // 2)

                wait_pos(act, blk_dn, f * NB)
                act.wait_ge(experts_in, 16 * 2)
                act.wait_ge(table_ready, f + 1)
                digits = [load_digits(act, 0)]
                for b in range(FETCH):
                    copy_down(b, b, expert_of(digits[0], b))
                evac_pair(0, 0)
                silu(0, 0)
                with_blocks(act, step)
                evac_y((NB - 1) // BU, (NB - 1) % BU)

            steps(lambda k: front(0, k), 1, 1)
            act.wait_ge(small_in, 16 * 5)
            nc.scalar.activation(decay[:, 1:2], decay[:, 0:1], ACT.Tanh, scale=0.5).then_inc(tanh_done, 1)
            experts(0)
            steps(middle, 1, 3)
            experts(1)
            for k in range(G):
                act.wait_ge(x3_done, k + 1)
                act.dma_start(out_dram[:, k * TPG:(k + 1) * TPG, :], tiles(xres, k)).then_inc(stored, 16)

        @block.vector
        def _(dve):
            def stats_of(kind, n, k):
                wait_pos(dve, stats[kind], n)
                for t in range(TPG):
                    last = nc.vector.bn_stats(st[kind][:, t, :], xres[:, k * TPG + t, :])
                last.then_inc(bn_done[kind], 1)
                dve.wait_ge(bn_done[kind], n + 1)
                for t in range(TPG):
                    last = nc.vector.bn_aggr(mv[kind][:, k * TPG + t, :], st[kind][:, t, :])
                last.then_inc(stats[kind], 1)

            def add_half(k, what, done):
                nc.vector.scalar_tensor_tensor(out=tiles(xres, k), in0=what, scalar=0.5, in1=tiles(xres, k),
                                               op0=ALU.mult, op1=ALU.add).then_inc(done, 1)

            def add_back(f, k, done):
                dve.wait_ge(back_in[k], 16 * (f + 1))
                add_half(k, tiles(back, k), done)

            def scan(k):
                dve.wait_ge(turned["a"], k + 1)
                wait_pos(dve, mixed, k - 1)
                nc.vector.tensor_tensor_scan(scanned[:, k % 2, :], keep[:], tp["a"][:], 0.0, ALU.mult,
                                             ALU.add).then_inc(scan_done, 1)

            def add_retrieved(k):
                dve.wait_ge(mixed, k + 1)
                dve.wait_ge(selfed, k + 1)
                nc.vector.tensor_tensor(tiles(xres, k), by_tile(o_ps[:]), tiles(xres, k), ALU.add).then_inc(x2_done, 1)
                dve.wait_ge(x2_done, k + 1)

            def mult(n, h):
                dve.wait_ge(silu_done, n * HH + h + 1)
                wait_pos(dve, down_done, n - 1)
                nc.vector.tensor_tensor(hs[:, n % 2, h, :], sg[:, h, :], u_ps[h][:], ALU.mult).then_inc(mult_done, 1)

            def add_shared(n, k):
                dve.wait_ge(down_done, n + 1)
                add_half(k, by_tile(o_ps[:]), half_done)

            def choose(n, q):
                step = [0]

                def link(ins):
                    step[0] += 1
                    ins.then_inc(route, 1)
                    dve.wait_ge(route, n * ROUTE_STEPS + step[0])

                lg, pr, one = by_tile(rt[:, LOG]), by_tile(prefer[:]), chosen[:, q, 0:TPG, :]
                dve.wait_ge(logits, n + 1)
                wait_pos(dve, route, n * ROUTE_STEPS)
                link(nc.vector.tensor_reduce(top[:], lg, AX.X, ALU.max))
                link(nc.vector.tensor_tensor(cand[:], lg, top[:].unsqueeze(2).to_broadcast([P, TPG, E]), ALU.is_ge))
                link(nc.vector.tensor_tensor(cand[:], cand[:], pr, ALU.mult))
                link(nc.vector.tensor_reduce(first[:], cand[:], AX.X, ALU.max))
                link(nc.vector.tensor_tensor(one, pr, first[:].unsqueeze(2).to_broadcast([P, TPG, E]), ALU.is_equal))
                with nc.allow_low_precision("whole numbers up to NT"):
                    nc.vector.tensor_reduce(chosen[:, 1 - q, TPG, :], chosen[:, q, :, :].rearrange("p t e -> p e t"),
                                            AX.X, ALU.add).then_inc(route, 1)

            def place_rows(n, k, q):
                dve.wait_ge(ranked, n + 1)
                wait_pos(dve, slotted, n)
                nc.vector.tensor_tensor(place[:], by_tile(rt[:, RANK]), chosen[:, q, 0:TPG, :],
                                        ALU.mult).then_inc(route, 1)
                dve.wait_ge(route, (n + 1) * ROUTE_STEPS)
                with nc.allow_low_precision("whole numbers"):
                    nc.vector.tensor_reduce(cols(slot, k), place[:], AX.X, ALU.add).then_inc(slotted, 1)

            def front(f, k):
                n, q = f * G + k, k % 2
                if f == 0 and valid(k + 2):
                    load = [i for i, (lo, hi) in enumerate(X_LOADS) if lo <= k + 2 < hi][0]
                    dve.wait_ge(x_in[load], 16)
                    stats_of("f", n + 2, k + 2)
                if valid(k):
                    choose(n, q)
                if valid(k - 1):
                    mult(n - 1, 0)
                if f == 1 and valid(k + 2):
                    add_retrieved(k + 2)
                    stats_of("f", n + 2, k + 2)
                if valid(k):
                    place_rows(n, k, q)
                if valid(k - 1):
                    mult(n - 1, 1)
                if k == G - 1:
                    pads_behind(f)
                if valid(k - 2):
                    add_shared(n - 2, k - 2)
                if k == G - 1:
                    tables(f)

            def middle(k):
                if valid(k + 3):
                    add_back(0, k + 3, x1_done)
                    dve.wait_ge(x1_done, k + 4)
                    stats_of("a", k + 3, k + 3)
                if valid(k + 2):
                    scan(k + 2)
                front(1, k)

            def pads_behind(f):
                dve.wait_ge(totals, f + 1)
                if f == 0:
                    dve.wait_ge(table_const, N_TABLE_CONST)
                wait_pos(dve, table_ready, f)
                nc.vector.tensor_tensor(pad_row[:], rt[:, TOT], pad_base[:], ALU.add).then_inc(pads_at, 1)

            def tables(f):
                step = [0]

                def link(ins):
                    step[0] += 1
                    ins.then_inc(tabs, 1)
                    dve.wait_ge(tabs, f * TAB_STEPS + step[0])

                tot = rt[:, TOT]
                link(nc.vector.tensor_scalar(n_up[:], tot, float(P - 1), None, ALU.add))
                link(nc.vector.tensor_scalar(n_blk[:], n_up[:], P.bit_length() - 1, None, ALU.logical_shift_right))
                link(nc.vector.tensor_copy(blk[:], n_blk[:]))
                link(nc.vector.tensor_tensor(blk_upto[:], upto[:], blk[:].unsqueeze(1).to_broadcast([P, E, E]),
                                             ALU.mult))
                link(nc.vector.tensor_reduce(blk_end[:], blk_upto[:], AX.X, ALU.add))
                link(nc.vector.tensor_scalar(last_blk[:], blk_end[:, E - 1:E], -1.0, None, ALU.add))
                link(nc.vector.tensor_scalar(real_blk[:], block_no[:], last_blk[:], None, ALU.min))
                link(nc.vector.tensor_tensor(past[:], real_blk[:].unsqueeze(2).to_broadcast([P, NBL, E]),
                                             blk_end[:].unsqueeze(1).to_broadcast([P, NBL, E]), ALU.is_ge))
                exps = blk_exp[:, BU - FETCH:BU - FETCH + NBL]
                link(nc.vector.tensor_reduce(exps, past[:], AX.X, ALU.add))
                link(nc.vector.tensor_tensor(past_n[:], past[:], blk[:].unsqueeze(1).to_broadcast([P, NBL, E]),
                                             ALU.mult))
                link(nc.vector.tensor_reduce(blk_from[:], past_n[:], AX.X, ALU.add))
                link(nc.vector.tensor_tensor(blk_from[:], real_blk[:], blk_from[:], ALU.subtract))
                link(nc.vector.tensor_scalar(blk_from[:], blk_from[:], float(P), None, ALU.mult))
                link(nc.vector.tensor_tensor(extra[:], block_no[:], real_blk[:], ALU.subtract))
                link(nc.vector.tensor_scalar(to_replica[:], extra[:], float(DUMP), None, ALU.mult))
                link(nc.vector.tensor_tensor(packed[:], blk_exp[:].rearrange("p (j s) -> p j s", s=BU),
                                             digit[:].unsqueeze(1).to_broadcast([P, LOADS + 1, BU]), ALU.mult))
                with nc.allow_low_precision("whole numbers below 2 ** 24"):
                    link(nc.vector.tensor_reduce(tab_exp[:], packed[:], AX.X, ALU.add))
                nc.vector.scalar_tensor_tensor(out=tab_row[:], in0=exps, scalar=float(CAP), in1=blk_from[:],
                                               op0=ALU.mult, op1=ALU.add).then_inc(table_ready, 1)

            def experts(f):
                def mul(b, r):
                    dve.wait_ge(blk_silu, f * NB + b + 1)
                    wait_pos(dve, blk_dn, f * NB + b - 1)
                    nc.vector.tensor_tensor(eh[:, r, :], eg[:, r, :], bank[4 + r][:, H:2 * H],
                                            ALU.mult).then_inc(blk_mul, 1)

                def copy_up(b, r, e):
                    wait_pos(dve, blk_gu, f * NB + b - WR + 1)
                    stand(dve)
                    nc.vector.tensor_copy(wgu[:, r, :], tile(gu, e)).then_inc(blk_wgu, 1)

                def step(j, s, more=True):
                    b = j * BU + s
                    if s == 0:
                        digits[0] = load_digits(dve, j + 1)
                    if more:
                        mul(b + 1, (s + 1) % 2)
                    if not is_int(j) or b + FETCH < NB:
                        copy_up(b + FETCH, (s + FETCH) % WR, expert_of(digits[0], s + FETCH))

                wait_pos(dve, blk_gu, f * NB)
                dve.wait_ge(experts_in, 16 * 2)
                dve.wait_ge(table_ready, f + 1)
                digits = [load_digits(dve, 0)]
                for b in range(FETCH):
                    copy_up(b, b, expert_of(digits[0], b))
                mul(0, 0)
                with_blocks(dve, step)

            steps(lambda k: front(0, k), 2, 2)
            dve.wait_ge(mix_raw, 1)
            nc.vector.tensor_scalar(mix[:], tp["a"][:, 0:C], gate[:], None, ALU.mult).then_inc(setup, 1)
            dve.wait_ge(tanh_done, 1)
            nc.vector.tensor_scalar(decay[:, 0:1], decay[:, 1:2], 0.5, 0.5, ALU.mult, ALU.add).then_inc(setup, 1)
            nc.vector.memset(keep[:], 1.0).then_inc(setup, 1)
            nc.vector.memset(chosen[:, 0, TPG, :], 0.0).then_inc(setup, 1)
            dve.wait_ge(setup, 4)
            nc.vector.tensor_scalar(keep[:], keep[:], decay[:, 0:1], None, ALU.mult).then_inc(setup, 1)
            dve.wait_ge(setup, 5)
            nc.vector.memset(keep[:].rearrange("p (b t) -> p b t", t=T)[:, :, 0], 0.0).then_inc(setup, 1)
            dve.wait_ge(setup, 6)
            experts(0)
            steps(middle, 2, 3)
            experts(1)
            for k in range(G):
                add_back(1, k, x3_done)

        @block.tensor
        def _(pe):
            def turn(kind, n, src, at, free):
                pe.wait_ge(normed[kind], n + 1)
                wait_pos(pe, free, n)
                for t in range(TPG):
                    last = nc.tensor.transpose(tp[kind][:, t * P:(t + 1) * P], src[:, at * TPG + t, 0:C], ident[:])
                last.then_inc(turned[kind], 1)

            def gate_up(n, h):
                pe.wait_ge(xnT_ready, n + 1)
                wait_pos(pe, mult_done, (n - 1) * HH + h + 1)
                for ps, at in ((g_ps[h], h * P), (u_ps[h], H + h * P)):
                    last = nc.tensor.matmul(ps[:], gu[:, SHARED, at:at + P], xnT[:, n % 2, :], start=True, stop=True)
                last.then_inc(gu_done, 1)

            def down(n):
                pe.wait_ge(mult_done, (n + 1) * HH)
                for t in range(TPG):
                    for h in range(HH):
                        last = nc.tensor.matmul(o_ps[:, t * C:(t + 1) * C], hs[:, n % 2, h, t * P:(t + 1) * P],
                                                dn[:, SHARED, h, :], start=(h == 0), stop=(h == HH - 1))
                last.then_inc(down_done, 1)

            def front(f, k):
                n, q = f * G + k, k % 2
                if valid(k):
                    turn("f", n, xn, k, xnT_ready)
                if valid(k - 1):
                    gate_up(n - 1, 0)
                if f == 1 and valid(k + 2):
                    turn("a", k + 2, xa, q, scan_done)
                if valid(k):
                    pe.wait_ge(xnT_ready, n + 1)
                    wait_pos(pe, route, n * ROUTE_STEPS)
                    for t in range(TPG):
                        last = nc.tensor.matmul(rt[:, t * E:(t + 1) * E], xnT[:, q, t * P:(t + 1) * P], routerT[:],
                                                start=True, stop=True)
                    last.then_inc(logits, 1)
                if valid(k - 1):
                    gate_up(n - 1, 1)
                if valid(k):
                    pe.wait_ge(route, n * ROUTE_STEPS + ROUTE_STEPS - 1)
                    if k == G - 1:
                        count_all()
                    ranks = by_tile(rt[:, RANK])
                    nc.tensor.matmul(ranks, before[:], chosen[:, q, 0:TPG, :], start=True, stop=False)
                    for t in range(TPG - 1):
                        nc.tensor.matmul(ranks[:, t + 1:TPG, :], ones[:],
                                         chosen[:, q, t:t + 1, :].to_broadcast([P, TPG - 1 - t, E]),
                                         start=False, stop=False)
                    nc.tensor.matmul(ranks, ones[:], chosen[:, q, TPG:TPG + 1, :].to_broadcast([P, TPG, E]),
                                     start=False, stop=False)
                    nc.tensor.matmul(ranks, ones[:], region[:].unsqueeze(1).to_broadcast([P, TPG, E]),
                                     start=False, stop=True).then_inc(ranked, 1)
                if f == 1 and valid(k + 2):
                    pe.wait_ge(scan_done, k + 3)
                    if valid(k - 3):
                        pe.wait_ge(half_done, n - 2)
                    for t in range(TPG):
                        last = nc.tensor.matmul(o_ps[:, t * C:(t + 1) * C], scanned[:, q, t * P:(t + 1) * P],
                                                mix[:], start=True, stop=True)
                    last.then_inc(mixed, 1)
                if valid(k - 2):
                    if f == 1 and valid(k + 2):
                        pe.wait_ge(x2_done, k + 3)
                    else:
                        wait_pos(pe, half_done, n - 2)
                    down(n - 2)

            def count_all():
                nc.tensor.matmul(rt[:, TOT], ones[:], chosen[:, G % 2, TPG, :], start=True,
                                 stop=True).then_inc(totals, 1)

            def experts(f):
                def turn_pair(j, pair):
                    n = f * LOADS * PAIRS + j * PAIRS + pair
                    wait_pos(pe, blk_xT, n - 1)
                    for s in (2 * pair, 2 * pair + 1):
                        pe.wait_ge(blk_in[s], (f * LOADS + j + 1) * 16)
                        last = nc.tensor.transpose(bank[pair % 2][:, s % 2 * P:(s % 2 + 1) * P], xs[:, s, 0:C],
                                                   ident[:])
                    last.then_inc(blk_turn, 1)

                def gate_up_block(j, s):
                    b = j * BU + s
                    pe.wait_ge(blk_xT, f * LOADS * PAIRS + j * PAIRS + s // 2 + 1)
                    pe.wait_ge(blk_wgu, f * NB + b + 1)
                    wait_pos(pe, blk_mul, f * NB + b - 1)
                    for i in range(2 * HH):
                        last = nc.tensor.matmul(bank[4 + s % 2][:, i * P:(i + 1) * P],
                                                wgu[:, s % WR, i * P:(i + 1) * P], xsT[:, s // 2 % 2, s % 2, :],
                                                start=True, stop=True)
                    last.then_inc(blk_gu, 1)

                def down_block(b, s):
                    pe.wait_ge(blk_mul, f * NB + b + 1)
                    pe.wait_ge(blk_wdn, f * NB + b + 1)
                    wait_pos(pe, blk_y, f * NB + b - 1)
                    for h in range(HH):
                        last = nc.tensor.matmul(bank[2 + s % 2][:, 0:C], eh[:, s % 2, h * P:(h + 1) * P],
                                                wdn[:, s % WR, h * C:(h + 1) * C],
                                                start=(h == 0), stop=(h == HH - 1))
                    last.then_inc(blk_dn, 1)

                def step(j, s, more=True):
                    if more:
                        gate_up_block(j + (s + 1) // BU, (s + 1) % BU)
                    down_block(j * BU + s, s)
                    if is_int(j) and j * BU + s == 0:
                        turn_pair(0, 1)
                    if s % 2 and ahead(j, s):
                        turn_pair(j + (s + 3) // BU, (s + 3) % BU // 2)

                pe.wait_ge(table_ready, f + 1)
                turn_pair(0, 0)
                pe.wait_ge(half_done, (f + 1) * G)
                gate_up_block(0, 0)
                with_blocks(pe, step)

            pe.wait_ge(const_made, N_CONST)
            pe.wait_ge(small_in, 16 * 5)
            nc.tensor.matmul(tp["a"][:, 0:C], hank_u[:], hank_b[:], start=True, stop=True).then_inc(mix_raw, 1)
            pe.wait_ge(shared_in, 16 * 2)
            steps(lambda k: front(0, k), 2, 0)
            pe.wait_ge(setup, 1)
            experts(0)
            pe.wait_ge(setup, 6)
            steps(lambda k: front(1, k), 2, 2)
            experts(1)


def kernel(L0_attn_x, L0_attn_bind_key, L0_attn_unbind_key, L0_attn_gate, L0_attn_decay, L0_ffn_up, L0_ffn_gate,
           L0_ffn_down, L0_ffn_router, L0_ffn_w_up_s, L0_ffn_w_gate_s, L0_ffn_w_down_s):
    import numpy as np
    import concourse.bacc as bacc
    from concourse.bass_utils import run_bass_kernel_spmd

    def a(x):
        return np.asarray(x)

    gates = np.concatenate([a(L0_ffn_gate), a(L0_ffn_w_gate_s)[None]], 0)
    ups = np.concatenate([a(L0_ffn_up), a(L0_ffn_w_up_s)[None]], 0)
    gu = np.concatenate([gates, ups], 1).transpose(2, 0, 1)
    downs = np.concatenate([a(L0_ffn_down), a(L0_ffn_w_down_s)[None]], 0)
    dn = downs.reshape(E + 1, C, HH, P).transpose(3, 0, 2, 1)
    arrays = {
        "x": a(L0_attn_x),
        "gu": gu,
        "dn": dn,
        "router": a(L0_ffn_router).T,
        "bind": np.concatenate([a(L0_attn_bind_key)] * 2),
        "unbind": np.concatenate([a(L0_attn_unbind_key)] * 2),
        "gate": a(L0_attn_gate).reshape(1),
        "decay": a(L0_attn_decay).reshape(1),
    }
    arrays = {name: np.ascontiguousarray(v) for name, v in arrays.items()}
    nc = bacc.Bacc("TRN2", target_bir_lowering=False, num_devices=1)
    ins = [nc.dram_tensor("in_" + name, v.shape, mybir.dt.from_np(v.dtype), kind="ExternalInput").ap()
           for name, v in arrays.items()]
    out = nc.dram_tensor("out", (B, T, C), F32, kind="ExternalOutput").ap()
    build(nc, *ins, out)
    r = run_bass_kernel_spmd(nc, [{"in_" + name: v for name, v in arrays.items()}], core_ids=[0])
    return r.results[0]["out"]
```

```python
from contextlib import ExitStack

import concourse.bass as bass
from concourse import mybir

ALU = mybir.AluOpType
ACT = mybir.ActivationFunctionType
AX = mybir.AxisListType
F32 = mybir.dt.float32
BF16 = mybir.dt.bfloat16
I32 = mybir.dt.int32

P = 128
C = 128
E = 8
SHARED = E
H = 256
HH = H // P
B, T = 16, 256
N = B * T
NT = N // P
TPG = 4
G = NT // TPG
GC = TPG * P
ROW = C + 4
CAP = N + P
X_LOADS = ((0, 1), (1, 2), (2, 4), (4, G))
AHEAD = 3
NB = NT + E - 1
NBL = NB + 1
BU = 8
PAIRS = BU // 2
LOADS = NBL // BU
WR = 4
FETCH = 3
DUMP = N + E * P
PADS_SP = 5
EPS = 1e-05

DOWN = HH
SHARED_PARTS = [(0, 0)] + [part for g in range(G) for part in ((g, 1), (g + 1, 0), (g, DOWN)) if part[0] < G]
PER_STEP = 2
EARLY = PER_STEP * (G - 1)
LATE = EARLY + 5

ROUTE_STEPS = 7
RSTD_STEPS = 2
N_CONST = 9
N_TABLE_CONST = 6 + BU


def slot_blocks(s):
    return len(range(s, NB, BU))


def is_int(j):
    return isinstance(j, int)


def pair_ahead(j, s):
    return not is_int(j) or j * BU + s + 3 < NBL


def with_blocks(eng, step):
    for s in range(BU):
        step(0, s)
    with eng.Fori(1, NB // BU) as j:
        for s in range(BU):
            step(j, s)
    for b in range(NB // BU * BU, NB):
        step(b // BU, b % BU, more=b + 1 < NB)


def build(nc, x_in, gu_in, dn_in, router_in, bind_in, unbind_in, gate_in, decay_in, out):
    x_dram = x_in.rearrange("b t c -> (b t) c").rearrange("(i p) c -> p i c", p=P)
    out_dram = out.rearrange("b t c -> (b t) c").rearrange("(i p) c -> p i c", p=P)
    dispatched = nc.dram_tensor("dispatched", [E * CAP, ROW], F32, kind="Internal")
    returned = nc.dram_tensor("returned", [DUMP * (E + 1), C], F32, kind="Internal")
    returned_tiles = returned[0:N, :].rearrange("(i p) c -> p i c", p=P)

    with ExitStack() as ctx:
        def sb(name, shape, dt=F32):
            return ctx.enter_context(nc.sbuf_tensor(name, shape, dt))

        def sem(name):
            return ctx.enter_context(nc.semaphore(name))

        gu = sb("gu", [P, E + 1, 2 * H])
        dn = sb("dn", [P, E + 1, HH, C])
        routerT = sb("routerT", [P, E])
        ident = sb("ident", [P, P])
        before = sb("before", [P, P], BF16)
        ones = sb("ones", [P, P], BF16)
        region = sb("region", [P, E], BF16)
        prefer = sb("prefer", [P, TPG * E])
        pad_base = sb("pad_base", [P, E])
        upto = sb("upto", [P, E, E])
        block_no = sb("block_no", [P, NBL])
        block_dump = sb("block_dump", [P, NBL])
        minus_half = sb("minus_half", [P, TPG])
        minus_one = sb("minus_one", [P, TPG])
        pads = sb("pads", [P, E, ROW])
        hank_b = sb("hank_b", [P, P])
        hank_u = sb("hank_u", [P, P])
        mix = sb("mix", [P, C])
        gate = sb("gate", [P, 1])
        decay = sb("decay", [P, 2])
        keep = sb("keep", [P, GC])

        xres = sb("xres", [P, NT, C])
        xn = sb("xn", [P, NT, ROW])
        xa = sb("xa", [P, 2 * TPG, C])
        back = sb("back", [P, NT, C])
        xnT = sb("xnT", [P, G, GC])
        scanned = sb("scanned", [P, 2, GC])
        st = {k: sb("st_" + k, [P, TPG, 6]) for k in "fa"}
        mv = {k: sb("mv_" + k, [P, NT, 2]) for k in "fa"}
        var = {k: sb("var_" + k, [P, NT]) for k in "fa"}
        minus_mean = {k: sb("minus_mean_" + k, [P, NT]) for k in "fa"}
        scale = {k: sb("scale_" + k, [P, NT]) for k in "fa"}
        shift = {k: sb("shift_" + k, [P, NT]) for k in "fa"}
        scale_more = sb("scale_more", [P, NT])

        top = sb("top", [P, TPG])
        cand = sb("cand", [P, TPG, E])
        first = sb("first", [P, TPG])
        chosen = sb("chosen", [P, 2, TPG + 1, E], BF16)
        place = sb("place", [P, TPG, E])
        slot = sb("slot", [P, NT], I32)
        pad_row = sb("pad_row", [P, E], I32)
        n_up = sb("n_up", [P, E], I32)
        n_blk = sb("n_blk", [P, E], I32)
        blk = sb("blk", [P, E])
        blk_upto = sb("blk_upto", [P, E, E])
        blk_end = sb("blk_end", [P, E])
        last_blk = sb("last_blk", [P, 1])
        real_blk = sb("real_blk", [P, NBL])
        past = sb("past", [P, NBL, E])
        past_n = sb("past_n", [P, NBL, E])
        blk_exp = sb("blk_exp", [P, (LOADS + 1) * BU])
        blk_from = sb("blk_from", [P, NBL])
        unused = sb("unused", [P, E])
        to_replica = sb("to_replica", [P, NBL], I32)
        digit = sb("digit", [P, BU])
        packed = sb("packed", [P, LOADS + 1, BU])
        tab_exp = sb("tab_exp", [P, LOADS + 1], I32)
        tab_row = sb("tab_row", [P, NBL], I32)

        sg = sb("sg", [P, HH, GC])
        hs = sb("hs", [P, 2, HH, GC])

        xs = sb("xs", [P, BU, ROW])
        token = sb("token", [P, BU], I32)
        xsT = sb("xsT", [P, 2, 2, P])
        eg = sb("eg", [P, WR, H])
        eh = sb("eh", [P, WR, H])
        wgu = sb("wgu", [P, WR, 2 * H])
        wdn = sb("wdn", [P, WR, HH * C])
        ey = sb("ey", [P, BU, C])

        bank = [ctx.enter_context(nc.psum_tensor(f"bank{i}", [P, GC], F32)) for i in range(8)]
        tp = {"f": bank[0], "a": bank[1]}
        rt = bank[2]
        o_ps = bank[3]
        g_ps, u_ps = [bank[4], bank[6]], [bank[5], bank[7]]
        LOG, RANK, TOT = slice(0, TPG * E), slice(TPG * E, 2 * TPG * E), slice(2 * TPG * E, (2 * TPG + 1) * E)

        const_made = sem("const_made")
        table_const = sem("table_const")
        const_chain = sem("const_chain")
        x_in = [sem(f"x_in{i}") for i in range(len(X_LOADS))]
        small_in = sem("small_in")
        shared_in, experts_in = sem("shared_in"), sem("experts_in")
        tanh_done, mix_raw = sem("tanh_done"), sem("mix_raw")
        setup = sem("setup")
        bn_done = {k: sem("bn_done_" + k) for k in "fa"}
        stats = {k: sem("stats_" + k) for k in "fa"}
        rstd_done = {k: sem("rstd_done_" + k) for k in "fa"}
        normed = {k: sem("normed_" + k) for k in "fa"}
        turned = {k: sem("turned_" + k) for k in "fa"}
        xnT_ready = sem("xnT_ready")
        logits = sem("logits")
        route = sem("route")
        ranked = sem("ranked")
        slotted = sem("slotted")
        sent = sem("sent")
        gu_done = sem("gu_done")
        silu_done, mult_done = sem("silu_done"), sem("mult_done")
        down_done, half_done = sem("down_done"), sem("half_done")
        totals = sem("totals")
        pads_at = sem("pads_at")
        tabs, table_ready = sem("tabs"), sem("table_ready")
        pad_sent = sem("pad_sent")
        back_in = [sem(f"back_in{k}") for k in range(G)]
        x1_done = sem("x1_done")
        scan_done, mixed = sem("scan_done"), sem("mixed")
        selfed, x2_done = sem("selfed"), sem("x2_done")
        blk_in = [sem(f"blk_in{s}") for s in range(BU)]
        blk_out = [sem(f"blk_out{s}") for s in range(BU)]
        blk_tok = sem("blk_tok")
        blk_turn, blk_xT = sem("blk_turn"), sem("blk_xT")
        blk_wgu, blk_wdn = sem("blk_wgu"), sem("blk_wdn")
        blk_gu, blk_silu, blk_mul = sem("blk_gu"), sem("blk_silu"), sem("blk_mul")
        blk_dn, blk_y = sem("blk_dn"), sem("blk_y")
        x3_done, stored = sem("x3_done"), sem("stored")

        block = ctx.enter_context(nc.Block())

        def tiles(buf, k):
            return buf[:, k * TPG:(k + 1) * TPG, :]

        def cols(buf, k):
            return buf[:, k * TPG:(k + 1) * TPG]

        def tile(buf, i):
            return buf[:, bass.ds(i, 1), :].rearrange("p a c -> p (a c)")

        def by_tile(ap):
            return ap.rearrange("p (t e) -> p t e", t=TPG)

        def valid(k):
            return 0 <= k < G

        def steps(body, ahead):
            for k in range(-ahead, G):
                body(k)

        def parts_at(k, i):
            return SHARED_PARTS[PER_STEP * (k - 1) + i:][:1] if 1 <= k < G else []

        def parts_done(last, down):
            return sum((part == DOWN) == down for g, part in SHARED_PARTS[:last])

        def expert_of(digits, b):
            return digits >> 3 * ((b - FETCH) % BU) & E - 1

        def load_digits(eng, i):
            return eng.value_load(tab_exp[0:1, bass.ds(i, 1)], min_val=0, max_val=E ** BU - 1)

        def send_pads(eng, experts):
            for e in experts:
                row = eng.value_load(pad_row[0:1, e:e + 1], min_val=0, max_val=E * CAP - P)
                eng.dma_start(dispatched[bass.ds(row, P), :], pads[:, e, :]).then_inc(pad_sent, 16)

        def stand(eng):
            eng.nop(nofuse=True)

        def wait_pos(eng, s, value):
            if not (is_int(value) and value <= 0):
                eng.wait_ge(s, value)

        @block.sync
        def _(sp):
            def load_x(i):
                lo, hi = X_LOADS[i]
                sp.dma_start(xres[:, lo * TPG:hi * TPG, :], x_dram[:, lo * TPG:hi * TPG, :]).then_inc(x_in[i], 16)

            load_x(0)
            load_x(1)
            sp.dma_start(routerT[:], router_in).then_inc(small_in, 16)
            sp.dma_start(gu[:, SHARED, :], gu_in[:, SHARED, :]).then_inc(shared_in, 16)
            sp.dma_start(dn[:, SHARED, :, :], dn_in[:, SHARED, :, :]).then_inc(shared_in, 16)
            load_x(2)
            for key, hank in ((bind_in, hank_b), (unbind_in, hank_u)):
                windows = bass.AP(key.tensor, 0, [[1, P], [1, P]])
                sp.dma_start(hank[:], windows).then_inc(small_in, 16)
            sp.dma_start(gate[:], gate_in.partition_broadcast(P)).then_inc(small_in, 16)
            sp.dma_start(decay[:, 0:1], decay_in.partition_broadcast(P)).then_inc(small_in, 16)
            load_x(3)
            sp.dma_start(gu[:, 0:E, :], gu_in[:, 0:E, :]).then_inc(experts_in, 16)
            sp.dma_start(dn[:, 0:E, :, :], dn_in[:, 0:E, :, :]).then_inc(experts_in, 16)

            def block_row(b):
                return sp.value_load(tab_row[0:1, bass.ds(b, 1)], min_val=0, max_val=E * CAP - P)

            def load_block(f, j, s, row=None):
                b = j * BU + s
                wait_pos(sp, blk_turn, f * (NBL // 2) + (j - 1) * PAIRS + s // 2 + 1)
                stand(sp)
                first_use = is_int(j) and j == 0
                wait_pos(sp, blk_tok, f * NB if first_use else f * NB + b - BU + 1)
                stand(sp)
                if row is None:
                    row = block_row(b)
                sp.dma_start(xs[:, s, :], dispatched[bass.ds(row, P), :]).then_inc(blk_in[s], 16)

            sp.wait_ge(table_const, N_TABLE_CONST)
            for f in range(2):
                sp.wait_ge(pads_at, f + 1)
                send_pads(sp, range(0, PADS_SP))
                sp.wait_ge(table_ready, f + 1)
                rows = [block_row(b) for b in range(2)]
                sp.wait_ge(pad_sent, 16 * E * (f + 1))
                sp.wait_ge(sent, 16 * NT * (f + 1))
                for s in range(BU):
                    load_block(f, 0, s, rows[s] if s < 2 else None)
                with sp.Fori(1, LOADS) as j:
                    for s in range(BU):
                        load_block(f, j, s)
                for s in range(BU):
                    sp.wait_ge(blk_out[s], 16 * slot_blocks(s) * (f + 1))
                for k in range(G):
                    sp.dma_start(tiles(back, k),
                                 returned_tiles[:, k * TPG:(k + 1) * TPG, :]).then_inc(back_in[k], 16)
            sp.wait_ge(stored, 16 * G)

        @block.gpsimd
        def _(pool):
            chained = [0]
            small = dict(allow_small_or_imprecise_dtypes=True)

            def chain(ins):
                chained[0] += 1
                ins.then_inc(const_chain, 1)
                pool.wait_ge(const_chain, chained[0])

            chain(nc.gpsimd.memset(ident[:], 0.0))
            nc.gpsimd.affine_select(out=ident[:], in_=ident[:], compare_op=ALU.not_equal, fill=1.0, base=0,
                                    pattern=[[-1, P]], channel_multiplier=1).then_inc(const_made, 1)
            nc.gpsimd.memset(minus_half[:], -0.5).then_inc(const_made, 1)
            nc.gpsimd.memset(minus_one[:], -1.0).then_inc(const_made, 1)
            nc.gpsimd.iota(xn[:, :, C:C + 1].bitcast(I32), [[P, NT], [0, 1]], base=0, channel_multiplier=1,
                           **small).then_inc(const_made, 1)
            last_row = pool.to_reg(E * CAP - 1)
            last_back = pool.to_reg(DUMP * (E + 1) - 1)

            def rstd(kind, n, k):
                s = rstd_done[kind]
                pool.wait_ge(stats[kind], n + 1)
                sc = cols(scale[kind], k)
                nc.gpsimd.tensor_tensor(sc, cols(var[kind], k), minus_half[:], ALU.pow).then_inc(s, 1)
                pool.wait_ge(s, n * RSTD_STEPS + 1)
                if kind == "a":
                    nc.gpsimd.tensor_tensor(cols(scale_more, k), sc, minus_one[:], ALU.subtract)
                nc.gpsimd.tensor_tensor(cols(shift[kind], k), sc, cols(minus_mean[kind], k),
                                        ALU.mult).then_inc(s, 1)

            def scatter(f, k):
                pool.wait_ge(slotted, f * G + k + 1)
                for i in range(k * TPG, (k + 1) * TPG):
                    nc.gpsimd.indirect_dma_start(
                        dispatched[:, :], bass.IndirectOffsetOnAxis(slot[:, i:i + 1], 0),
                        xn[:, i, :], None, bounds_check=last_row).then_inc(sent, 16)

            def first_ffn(k):
                if valid(k + AHEAD):
                    rstd("f", k + AHEAD, k + AHEAD)
                if valid(k):
                    scatter(0, k)

            def middle(k):
                if valid(k + 4):
                    rstd("a", k + 4, k + 4)
                if valid(k + 2):
                    rstd("f", G + k + 2, k + 2)
                if valid(k):
                    scatter(1, k)

            def experts(f):
                def tokens(j, s):
                    pool.wait_ge(blk_in[s], (f * LOADS + j + 1) * 16)
                    wait_pos(pool, blk_out[s], (f * slot_blocks(s) + j) * 16)
                    nc.gpsimd.tensor_tensor(token[:, s:s + 1], xs[:, s, C:C + 1].bitcast(I32),
                                            to_replica[:, bass.ds(j * BU + s, 1)], ALU.add).then_inc(blk_tok, 1)

                def send(j, s):
                    pool.wait_ge(blk_tok, f * NB + j * BU + s + 1)
                    pool.wait_ge(blk_y, f * NB + j * BU + s + 1)
                    stand(pool)
                    nc.gpsimd.indirect_dma_start(
                        returned[:, :], bass.IndirectOffsetOnAxis(token[:, s:s + 1], 0),
                        ey[:, s, :], None, bounds_check=last_back).then_inc(blk_out[s], 16)

                def step(j, s, more=True):
                    if more:
                        tokens(j + (s + 1) // BU, (s + 1) % BU)
                    send(j, s)

                pool.wait_ge(table_ready, f + 1)
                tokens(0, 0)
                with_blocks(pool, step)

            pool.wait_ge(const_made, 3)
            first_ffn(-AHEAD)
            nc.gpsimd.memset(xn[:, :, C + 1:ROW], 0.0).then_inc(const_made, 1)
            chain(nc.gpsimd.memset(ones[:], 1.0))
            nc.gpsimd.affine_select(out=before[:], in_=ones[:], compare_op=ALU.is_gt, fill=0.0, base=0,
                                    pattern=[[1, P]], channel_multiplier=-1).then_inc(const_made, 1)
            nc.gpsimd.iota(by_tile(prefer[:]), [[0, TPG], [-1, E]], base=E, channel_multiplier=0,
                           **small).then_inc(const_made, 1)
            nc.gpsimd.iota(region[:], [[CAP // P, E]], base=0, channel_multiplier=0, **small).then_inc(const_made, 1)
            nc.gpsimd.memset(chosen[:, 0, TPG, :], 0.0).then_inc(const_made, 1)
            for k in range(1 - AHEAD, 1):
                first_ffn(k)
            nc.gpsimd.iota(pad_base[:], [[CAP, E]], base=0, channel_multiplier=0, **small).then_inc(table_const, 1)
            nc.gpsimd.iota(block_no[:], [[1, NBL]], base=0, channel_multiplier=0, **small).then_inc(table_const, 1)
            nc.gpsimd.iota(block_dump[:], [[DUMP, NBL]], base=0, channel_multiplier=0,
                           **small).then_inc(table_const, 1)
            nc.gpsimd.memset(blk_exp[:], 0.0).then_inc(table_const, 1)
            for u in range(BU):
                nc.gpsimd.memset(digit[:, u:u + 1], float(E ** u)).then_inc(table_const, 1)
            chain(nc.gpsimd.memset(upto[:], 1.0))
            nc.gpsimd.affine_select(out=upto[:], in_=upto[:], compare_op=ALU.is_ge, fill=0.0, base=0,
                                    pattern=[[1, E], [-1, E]], channel_multiplier=0).then_inc(table_const, 1)
            chain(nc.gpsimd.memset(pads[:], 0.0))
            nc.gpsimd.iota(pads[:, :, C:C + 1].bitcast(I32), [[P, E], [0, 1]], base=N, channel_multiplier=1,
                           **small).then_inc(table_const, 1)
            for k in range(1, G):
                first_ffn(k)
            experts(0)
            steps(middle, 4)
            experts(1)

        @block.scalar
        def _(act):
            def norm(kind, n, k, dst, at):
                act.wait_ge(rstd_done[kind], (n + 1) * RSTD_STEPS)
                for t in range(TPG):
                    i = k * TPG + t
                    nc.scalar.activation(dst[:, at * TPG + t, 0:C], xres[:, i, :], ACT.Identity,
                                         bias=shift[kind][:, i:i + 1],
                                         scale=scale[kind][:, i:i + 1]).then_inc(normed[kind], 1)

            def add_self(k):
                act.wait_ge(normed["a"], (k + 1) * TPG)
                for i in range(k * TPG, (k + 1) * TPG):
                    last = nc.scalar.activation(xres[:, i, :], xres[:, i, :], ACT.Identity,
                                                bias=shift["a"][:, i:i + 1], scale=scale_more[:, i:i + 1])
                last.then_inc(selfed, 1)

            def evac_rows(n):
                act.wait_ge(turned["f"], n + 1)
                wait_pos(act, gu_done, (n - G + 1) * HH)
                nc.scalar.activation(xnT[:, n % G, :], tp["f"][:], ACT.Copy).then_inc(xnT_ready, 1)

            def shared(f, g, part):
                if part < HH:
                    silu_half(f * G + g, part)

            def silu_half(n, h):
                act.wait_ge(gu_done, n * HH + h + 1)
                wait_pos(act, mult_done, (n - 1) * HH + h + 1)
                nc.scalar.activation(sg[:, h, :], g_ps[h][:], ACT.Silu).then_inc(silu_done, 1)

            def front(f, k):
                n = f * G + k
                if valid(k):
                    evac_rows(n)
                if f == 1 and valid(k + 2):
                    add_self(k + 2)
                if valid(k + 1):
                    norm("f", n + 1, k + 1, xn, k + 1)
                for g, part in parts_at(k, 0):
                    shared(f, g, part)
                if f == 1 and valid(k + 3):
                    wait_pos(act, turned["a"], k + 2)
                    norm("a", k + 3, k + 3, xa, (k + 3) % 2)
                for g, part in parts_at(k, 1):
                    shared(f, g, part)
                if k == G - 1:
                    act.wait_ge(pads_at, f + 1)
                    send_pads(act, range(PADS_SP, E))

            def copy_up(f, b, r, e):
                wait_pos(act, blk_gu, f * NB + b - WR + 1)
                stand(act)
                nc.scalar.activation(wgu[:, r, :], tile(gu, e), ACT.Copy).then_inc(blk_wgu, 1)

            def before_experts(f):
                for g, part in SHARED_PARTS[EARLY:LATE - 1]:
                    shared(f, g, part)
                wait_pos(act, blk_gu, f * NB)
                act.wait_ge(experts_in, 16 * 2)
                act.wait_ge(table_ready, f + 1)
                digits = load_digits(act, 0)
                for b in range(FETCH):
                    copy_up(f, b, b, expert_of(digits, b))
                shared(f, *SHARED_PARTS[LATE - 1])

            def experts(f):
                def evac_pair(j, pair):
                    act.wait_ge(blk_turn, f * LOADS * PAIRS + j * PAIRS + pair + 1)
                    n = j * BU + pair * 2 - 2
                    wait_pos(act, blk_gu, f * NB if is_int(n) and n < 2 else f * NB + n)
                    nc.scalar.activation(xsT[:, pair % 2, :, :],
                                         bank[pair % 2][:, 0:2 * P].rearrange("p (s c) -> p s c", s=2),
                                         ACT.Copy).then_inc(blk_xT, 1)

                def silu(b, r):
                    act.wait_ge(blk_gu, f * NB + b + 1)
                    wait_pos(act, blk_mul, f * NB + b - WR + 1)
                    nc.scalar.activation(eg[:, r, :], bank[4 + r][:, 0:H], ACT.Silu).then_inc(blk_silu, 1)

                def step(j, s, more=True):
                    b = j * BU + s
                    if s == 0:
                        digits[0] = load_digits(act, j + 1)
                    if more:
                        silu(b + 1, (s + 1) % WR)
                    if is_int(j) and b == 0:
                        evac_pair(0, 1)
                    if not is_int(j) or b + FETCH < NB:
                        copy_up(f, b + FETCH, (s + FETCH) % WR, expert_of(digits[0], s + FETCH))
                    if s % 2 and pair_ahead(j, s):
                        evac_pair(j + (s + 3) // BU, (s + 3) % BU // 2)

                digits = [None]
                evac_pair(0, 0)
                silu(0, 0)
                with_blocks(act, step)

            def first_ffn(k):
                front(0, k)
                if k == 0:
                    act.wait_ge(small_in, 16 * 5)
                    nc.scalar.activation(decay[:, 1:2], decay[:, 0:1], ACT.Tanh, scale=0.5).then_inc(tanh_done, 1)

            steps(first_ffn, 1)
            before_experts(0)
            experts(0)
            for g, part in SHARED_PARTS[LATE:]:
                shared(0, g, part)
            steps(lambda k: front(1, k), 3)
            before_experts(1)
            experts(1)
            for g, part in SHARED_PARTS[LATE:]:
                shared(1, g, part)
            for k in range(G):
                act.wait_ge(x3_done, k + 1)
                act.dma_start(out_dram[:, k * TPG:(k + 1) * TPG, :], tiles(xres, k)).then_inc(stored, 16)

        @block.vector
        def _(dve):
            def stats_of(kind, n, k):
                wait_pos(dve, stats[kind], n)
                for t in range(TPG):
                    moments(kind, k, t)
                aggregate(kind, n, k)

            def moments(kind, k, t):
                nc.vector.bn_stats(st[kind][:, t, :], xres[:, k * TPG + t, :]).then_inc(bn_done[kind], 1)

            def aggregate(kind, n, k):
                done, m = bn_done[kind], tiles(mv[kind], k)
                dve.wait_ge(done, n * (TPG + 1) + TPG)
                for t in range(TPG):
                    last = nc.vector.bn_aggr(m[:, t, :], st[kind][:, t, :])
                last.then_inc(done, 1)
                dve.wait_ge(done, (n + 1) * (TPG + 1))
                nc.vector.tensor_scalar(cols(var[kind], k), m[:, :, 1], EPS, None, ALU.add)
                nc.vector.tensor_scalar(cols(minus_mean[kind], k), m[:, :, 0], -1.0, None,
                                        ALU.mult).then_inc(stats[kind], 1)

            def add_half(k, what, done):
                nc.vector.scalar_tensor_tensor(out=tiles(xres, k), in0=what, scalar=0.5, in1=tiles(xres, k),
                                               op0=ALU.mult, op1=ALU.add).then_inc(done, 1)

            def add_back(f, k, done):
                dve.wait_ge(back_in[k], 16 * (f + 1))
                dve.wait_ge(half_done, f * G + k + 1)
                add_half(k, tiles(back, k), done)

            def scan(k):
                dve.wait_ge(turned["a"], k + 1)
                wait_pos(dve, mixed, k - 1)
                nc.vector.tensor_tensor_scan(scanned[:, k % 2, :], keep[:], tp["a"][:], 0.0, ALU.mult,
                                             ALU.add).then_inc(scan_done, 1)

            def add_retrieved(k):
                dve.wait_ge(mixed, k + 1)
                dve.wait_ge(selfed, k + 1)
                nc.vector.tensor_tensor(tiles(xres, k), by_tile(tp["a"][:]), tiles(xres, k),
                                        ALU.add).then_inc(x2_done, 1)
                dve.wait_ge(x2_done, k + 1)

            def shared(f, g, part):
                if part < HH:
                    mult(f * G + g, part)
                else:
                    add_shared(f * G + g, g)

            def mult(n, h):
                dve.wait_ge(silu_done, n * HH + h + 1)
                wait_pos(dve, down_done, n - 1)
                nc.vector.tensor_tensor(hs[:, n % 2, h, :], sg[:, h, :], u_ps[h][:], ALU.mult).then_inc(mult_done, 1)

            def add_shared(n, k):
                dve.wait_ge(down_done, n + 1)
                add_half(k, by_tile(o_ps[:]), half_done)

            def choose(n, q, kind, m, k):
                step = [0]

                def link(ins):
                    step[0] += 1
                    ins.then_inc(route, 1)
                    if valid(k) and step[0] <= TPG:
                        moments(kind, k, step[0] - 1)
                    dve.wait_ge(route, n * ROUTE_STEPS + step[0])

                lg, pr, one = by_tile(rt[:, LOG]), by_tile(prefer[:]), chosen[:, q, 0:TPG, :]
                dve.wait_ge(logits, n + 1)
                wait_pos(dve, route, n * ROUTE_STEPS)
                if valid(k):
                    wait_pos(dve, stats[kind], m)
                link(nc.vector.tensor_reduce(top[:], lg, AX.X, ALU.max))
                link(nc.vector.tensor_tensor(cand[:], lg, top[:].unsqueeze(2).to_broadcast([P, TPG, E]), ALU.is_ge))
                link(nc.vector.tensor_tensor(cand[:], cand[:], pr, ALU.mult))
                link(nc.vector.tensor_reduce(first[:], cand[:], AX.X, ALU.max))
                link(nc.vector.tensor_tensor(one, pr, first[:].unsqueeze(2).to_broadcast([P, TPG, E]), ALU.is_equal))
                with nc.allow_low_precision("whole numbers up to NT"):
                    nc.vector.tensor_reduce(chosen[:, 1 - q, TPG, :], chosen[:, q, :, :].rearrange("p t e -> p e t"),
                                            AX.X, ALU.add).then_inc(route, 1)
                if valid(k):
                    aggregate(kind, m, k)

            def place_rows(n, k, q):
                dve.wait_ge(ranked, n + 1)
                wait_pos(dve, slotted, n)
                nc.vector.tensor_tensor(place[:], by_tile(rt[:, RANK]), chosen[:, q, 0:TPG, :],
                                        ALU.mult).then_inc(route, 1)
                dve.wait_ge(route, (n + 1) * ROUTE_STEPS)
                with nc.allow_low_precision("whole numbers"):
                    nc.vector.tensor_reduce(cols(slot, k), place[:], AX.X, ALU.add).then_inc(slotted, 1)

            def front(f, k):
                n, q = f * G + k, k % 2
                kind, later = ("f", k + AHEAD) if f == 0 else ("a", k + 4)
                if f == 0 and valid(later):
                    load = [i for i, (lo, hi) in enumerate(X_LOADS) if lo <= later < hi][0]
                    dve.wait_ge(x_in[load], 16)
                if valid(k):
                    choose(n, q, kind, later, later)
                elif f == 0 and valid(later):
                    stats_of(kind, later, later)
                for g, part in parts_at(k, 0):
                    shared(f, g, part)
                if f == 1 and valid(k + 2):
                    add_retrieved(k + 2)
                    stats_of("f", n + 2, k + 2)
                if valid(k):
                    place_rows(n, k, q)
                if k == G - 1:
                    pads_behind(f)
                for g, part in parts_at(k, 1):
                    shared(f, g, part)

            def before_experts(f):
                block_experts()
                tables()
                for g, part in SHARED_PARTS[EARLY:LATE - 1]:
                    shared(f, g, part)
                first_weights(f)
                shared(f, *SHARED_PARTS[LATE - 1])

            def add_first(k):
                if valid(k + 4):
                    add_back(0, k + 4, x1_done)
                    dve.wait_ge(x1_done, k + 5)
                    if k < 0:
                        stats_of("a", k + 4, k + 4)

            def middle(k):
                if valid(k + 2):
                    scan(k + 2)
                add_first(k)
                front(1, k)
                if k < -2:
                    shared(0, *SHARED_PARTS[k + 2])

            def pads_behind(f):
                dve.wait_ge(totals, f + 1)
                if f == 0:
                    dve.wait_ge(table_const, N_TABLE_CONST)
                wait_pos(dve, table_ready, f)
                nc.vector.tensor_tensor(pad_row[:], rt[:, TOT], pad_base[:], ALU.add).then_inc(pads_at, 1)

            tab_steps = [0]

            def link(ins):
                tab_steps[0] += 1
                ins.then_inc(tabs, 1)
                dve.wait_ge(tabs, tab_steps[0])

            def block_experts():
                tot = rt[:, TOT]
                link(nc.vector.tensor_scalar(n_up[:], tot, float(P - 1), None, ALU.add))
                link(nc.vector.tensor_scalar(n_blk[:], n_up[:], P.bit_length() - 1, None, ALU.logical_shift_right))
                link(nc.vector.tensor_copy(blk[:], n_blk[:]))
                link(nc.vector.tensor_tensor(blk_upto[:], upto[:], blk[:].unsqueeze(1).to_broadcast([P, E, E]),
                                             ALU.mult))
                link(nc.vector.tensor_reduce(blk_end[:], blk_upto[:], AX.X, ALU.add))
                link(nc.vector.tensor_scalar(last_blk[:], blk_end[:, E - 1:E], -1.0, None, ALU.add))
                link(nc.vector.tensor_scalar(real_blk[:], block_no[:], last_blk[:], None, ALU.min))
                link(nc.vector.tensor_tensor(past[:], real_blk[:].unsqueeze(2).to_broadcast([P, NBL, E]),
                                             blk_end[:].unsqueeze(1).to_broadcast([P, NBL, E]), ALU.is_ge))
                link(nc.vector.tensor_reduce(blk_exp[:, BU - FETCH:BU - FETCH + NBL], past[:], AX.X, ALU.add))
                link(nc.vector.tensor_scalar(unused[:], blk[:], float(-P), float(CAP), ALU.mult, ALU.add))

            def tables():
                link(nc.vector.tensor_tensor(past_n[:], past[:], unused[:].unsqueeze(1).to_broadcast([P, NBL, E]),
                                             ALU.mult))
                link(nc.vector.tensor_reduce(blk_from[:], past_n[:], AX.X, ALU.add))
                link(nc.vector.scalar_tensor_tensor(out=to_replica[:], in0=real_blk[:], scalar=float(-DUMP),
                                                    in1=block_dump[:], op0=ALU.mult, op1=ALU.add))
                link(nc.vector.tensor_tensor(packed[:], blk_exp[:].rearrange("p (j s) -> p j s", s=BU),
                                             digit[:].unsqueeze(1).to_broadcast([P, LOADS + 1, BU]), ALU.mult))
                with nc.allow_low_precision("whole numbers below 2 ** 24"):
                    link(nc.vector.tensor_reduce(tab_exp[:], packed[:], AX.X, ALU.add))
                nc.vector.scalar_tensor_tensor(out=tab_row[:], in0=real_blk[:], scalar=float(P), in1=blk_from[:],
                                               op0=ALU.mult, op1=ALU.add).then_inc(table_ready, 1)

            def copy_down(f, b, r, e):
                wait_pos(dve, blk_dn, f * NB + b - WR + 1)
                stand(dve)
                nc.vector.tensor_copy(wdn[:, r, :], tile(dn[:].rearrange("p e h c -> p e (h c)"),
                                                         e)).then_inc(blk_wdn, 1)

            def first_weights(f):
                wait_pos(dve, blk_dn, f * NB)
                dve.wait_ge(experts_in, 16 * 2)
                dve.wait_ge(table_ready, f + 1)
                digits = load_digits(dve, 0)
                for b in range(FETCH):
                    copy_down(f, b, b, expert_of(digits, b))

            def experts(f):
                def mul(b, r):
                    dve.wait_ge(blk_silu, f * NB + b + 1)
                    wait_pos(dve, blk_dn, f * NB + b - WR + 1)
                    nc.vector.tensor_tensor(eh[:, r, :], eg[:, r, :], bank[4 + r][:, H:2 * H],
                                            ALU.mult).then_inc(blk_mul, 1)

                def evac_y(j, s):
                    dve.wait_ge(blk_dn, f * NB + j * BU + s + 1)
                    wait_pos(dve, blk_out[s], 16 * (f * slot_blocks(s) + j))
                    nc.vector.tensor_copy(ey[:, s, :], bank[2 + s % 2][:, 0:C]).then_inc(blk_y, 1)

                def step(j, s, more=True):
                    b = j * BU + s
                    if s == 0:
                        digits[0] = load_digits(dve, j + 1)
                    if not is_int(j) or b > 1:
                        evac_y(j + (s - 2) // BU, (s - 2) % BU)
                    if more:
                        mul(b + 1, (s + 1) % WR)
                    if not is_int(j) or b + FETCH < NB:
                        copy_down(f, b + FETCH, (s + FETCH) % WR, expert_of(digits[0], s + FETCH))

                digits = [None]
                mul(0, 0)
                with_blocks(dve, step)
                for b in range(NB - 2, NB):
                    evac_y(b // BU, b % BU)

            def prepare_attention():
                dve.wait_ge(mix_raw, 1)
                nc.vector.tensor_scalar(mix[:], tp["a"][:, 0:C], gate[:], None, ALU.mult).then_inc(setup, 1)
                dve.wait_ge(tanh_done, 1)
                nc.vector.tensor_scalar(decay[:, 0:1], decay[:, 1:2], 0.5, 0.5, ALU.mult, ALU.add).then_inc(setup, 1)
                nc.vector.memset(keep[:], 1.0).then_inc(setup, 1)
                dve.wait_ge(setup, 3)
                nc.vector.tensor_scalar(keep[:], keep[:], decay[:, 0:1], None, ALU.mult).then_inc(setup, 1)
                dve.wait_ge(setup, 4)
                nc.vector.memset(keep[:].rearrange("p (b t) -> p b t", t=T)[:, :, 0], 0.0).then_inc(setup, 1)
                dve.wait_ge(setup, 5)

            def first_ffn(k):
                front(0, k)
                if k == 0:
                    prepare_attention()

            steps(first_ffn, AHEAD)
            before_experts(0)
            nc.vector.memset(chosen[:, 0, TPG, :], 0.0).then_inc(setup, 1)
            experts(0)
            for g, part in SHARED_PARTS[LATE:-2]:
                shared(0, g, part)
            steps(middle, 4)
            before_experts(1)
            experts(1)
            for g, part in SHARED_PARTS[LATE:-2]:
                shared(1, g, part)
            for k in range(G):
                add_back(1, k, x3_done)
                if k < 2:
                    shared(1, *SHARED_PARTS[k - 2])

        @block.tensor
        def _(pe):
            def turn(kind, n, src, at, free):
                wait_pos(pe, free, n)
                for t in range(TPG):
                    pe.wait_ge(normed[kind], n * TPG + t + 1)
                    last = nc.tensor.transpose(tp[kind][:, t * P:(t + 1) * P], src[:, at * TPG + t, 0:C], ident[:])
                last.then_inc(turned[kind], 1)

            def shared(f, g, part):
                n = f * G + g
                if part < HH:
                    gate_up(n, g, part)
                else:
                    down(n)

            def gate_up(n, g, h):
                pe.wait_ge(xnT_ready, n + 1)
                wait_pos(pe, mult_done, (n - 1) * HH + h + 1)
                for ps, at in ((g_ps[h], h * P), (u_ps[h], H + h * P)):
                    last = nc.tensor.matmul(ps[:], gu[:, SHARED, at:at + P], xnT[:, g, :], start=True, stop=True)
                last.then_inc(gu_done, 1)

            def down(n):
                pe.wait_ge(mult_done, (n + 1) * HH)
                wait_pos(pe, half_done, n)
                for t in range(TPG):
                    for h in range(HH):
                        last = nc.tensor.matmul(o_ps[:, t * C:(t + 1) * C], hs[:, n % 2, h, t * P:(t + 1) * P],
                                                dn[:, SHARED, h, :], start=(h == 0), stop=(h == HH - 1))
                last.then_inc(down_done, 1)

            def front(f, k):
                n, q = f * G + k, k % 2
                for g, part in parts_at(k, 0):
                    shared(f, g, part)
                if valid(k):
                    pe.wait_ge(xnT_ready, n + 1)
                    wait_pos(pe, route, n * ROUTE_STEPS)
                    for t in range(TPG):
                        last = nc.tensor.matmul(rt[:, t * E:(t + 1) * E], xnT[:, k, t * P:(t + 1) * P], routerT[:],
                                                start=True, stop=True)
                    last.then_inc(logits, 1)
                if f == 1 and valid(k + 2):
                    pe.wait_ge(scan_done, k + 3)
                    for t in range(TPG):
                        last = nc.tensor.matmul(tp["a"][:, t * C:(t + 1) * C], scanned[:, q, t * P:(t + 1) * P],
                                                mix[:], start=True, stop=True)
                    last.then_inc(mixed, 1)
                for g, part in parts_at(k, 1):
                    shared(f, g, part)
                if valid(k + 1):
                    turn("f", n + 1, xn, k + 1, xnT_ready)
                if valid(k):
                    pe.wait_ge(route, n * ROUTE_STEPS + ROUTE_STEPS - 1)
                    if k == G - 1:
                        count_all()
                    ranks = by_tile(rt[:, RANK])
                    nc.tensor.matmul(ranks, before[:], chosen[:, q, 0:TPG, :], start=True, stop=False)
                    for t in range(TPG - 1):
                        nc.tensor.matmul(ranks[:, t + 1:TPG, :], ones[:],
                                         chosen[:, q, t:t + 1, :].to_broadcast([P, TPG - 1 - t, E]),
                                         start=False, stop=False)
                    nc.tensor.matmul(ranks, ones[:], chosen[:, q, TPG:TPG + 1, :].to_broadcast([P, TPG, E]),
                                     start=False, stop=False)
                    nc.tensor.matmul(ranks, ones[:], region[:].unsqueeze(1).to_broadcast([P, TPG, E]),
                                     start=False, stop=True).then_inc(ranked, 1)
                if f == 1 and valid(k + 3):
                    turn("a", k + 3, xa, 1 - q, x2_done)

            def count_all():
                nc.tensor.matmul(rt[:, TOT], ones[:], chosen[:, G % 2, TPG, :], start=True,
                                 stop=True).then_inc(totals, 1)

            def experts(f):
                def turn_pair(j, pair):
                    n = f * LOADS * PAIRS + j * PAIRS + pair
                    wait_pos(pe, blk_xT, n - 1)
                    for s in (2 * pair, 2 * pair + 1):
                        pe.wait_ge(blk_in[s], (f * LOADS + j + 1) * 16)
                        last = nc.tensor.transpose(bank[pair % 2][:, s % 2 * P:(s % 2 + 1) * P], xs[:, s, 0:C],
                                                   ident[:])
                    last.then_inc(blk_turn, 1)

                def gate_up_block(j, s):
                    b = j * BU + s
                    pe.wait_ge(blk_xT, f * LOADS * PAIRS + j * PAIRS + s // 2 + 1)
                    pe.wait_ge(blk_wgu, f * NB + b + 1)
                    wait_pos(pe, blk_mul, f * NB + b - WR + 1)
                    for i in range(2 * HH):
                        last = nc.tensor.matmul(bank[4 + s % WR][:, i * P:(i + 1) * P],
                                                wgu[:, s % WR, i * P:(i + 1) * P], xsT[:, s // 2 % 2, s % 2, :],
                                                start=True, stop=True)
                    last.then_inc(blk_gu, 1)

                def down_block(b, s):
                    pe.wait_ge(blk_mul, f * NB + b + 1)
                    pe.wait_ge(blk_wdn, f * NB + b + 1)
                    wait_pos(pe, blk_y, f * NB + b - 1)
                    for h in range(HH):
                        last = nc.tensor.matmul(bank[2 + s % 2][:, 0:C], eh[:, s % WR, h * P:(h + 1) * P],
                                                wdn[:, s % WR, h * C:(h + 1) * C],
                                                start=(h == 0), stop=(h == HH - 1))
                    last.then_inc(blk_dn, 1)

                def step(j, s, more=True):
                    if more:
                        gate_up_block(j + (s + 1) // BU, (s + 1) % BU)
                    if is_int(j) and j * BU + s == 0:
                        turn_pair(0, 1)
                    else:
                        down_block(j * BU + s - 1, (s - 1) % BU)
                    if s % 2 and pair_ahead(j, s):
                        turn_pair(j + (s + 3) // BU, (s + 3) % BU // 2)

                pe.wait_ge(table_ready, f + 1)
                turn_pair(0, 0)
                pe.wait_ge(half_done, f * G + parts_done(LATE, down=True))
                pe.wait_ge(mult_done, f * G * HH + parts_done(LATE, down=False))
                gate_up_block(0, 0)
                with_blocks(pe, step)
                down_block(NB - 1, (NB - 1) % BU)
                pe.wait_ge(blk_mul, (f + 1) * NB)
                pe.wait_ge(blk_y, (f + 1) * NB)

            pe.wait_ge(const_made, N_CONST)
            pe.wait_ge(small_in, 16 * 5)
            nc.tensor.matmul(tp["a"][:, 0:C], hank_u[:], hank_b[:], start=True, stop=True).then_inc(mix_raw, 1)
            pe.wait_ge(shared_in, 16 * 2)
            steps(lambda k: front(0, k), 1)
            for g, part in SHARED_PARTS[EARLY:LATE]:
                shared(0, g, part)
            pe.wait_ge(setup, 1)
            experts(0)
            for g, part in SHARED_PARTS[LATE:]:
                shared(0, g, part)
            pe.wait_ge(setup, 6)
            steps(lambda k: front(1, k), 3)
            for g, part in SHARED_PARTS[EARLY:LATE]:
                shared(1, g, part)
            experts(1)
            for g, part in SHARED_PARTS[LATE:]:
                shared(1, g, part)


def kernel(L0_attn_x, L0_attn_bind_key, L0_attn_unbind_key, L0_attn_gate, L0_attn_decay, L0_ffn_up, L0_ffn_gate,
           L0_ffn_down, L0_ffn_router, L0_ffn_w_up_s, L0_ffn_w_gate_s, L0_ffn_w_down_s):
    import numpy as np
    import concourse.bacc as bacc
    from concourse.bass_utils import run_bass_kernel_spmd

    def a(x):
        return np.asarray(x)

    gates = np.concatenate([a(L0_ffn_gate), a(L0_ffn_w_gate_s)[None]], 0)
    ups = np.concatenate([a(L0_ffn_up), a(L0_ffn_w_up_s)[None]], 0)
    gu = np.concatenate([gates, ups], 1).transpose(2, 0, 1)
    downs = np.concatenate([a(L0_ffn_down), a(L0_ffn_w_down_s)[None]], 0)
    dn = downs.reshape(E + 1, C, HH, P).transpose(3, 0, 2, 1)
    arrays = {
        "x": a(L0_attn_x),
        "gu": gu,
        "dn": dn,
        "router": a(L0_ffn_router).T,
        "bind": np.concatenate([a(L0_attn_bind_key)] * 2),
        "unbind": np.concatenate([a(L0_attn_unbind_key)] * 2),
        "gate": a(L0_attn_gate).reshape(1),
        "decay": a(L0_attn_decay).reshape(1),
    }
    arrays = {name: np.ascontiguousarray(v) for name, v in arrays.items()}
    nc = bacc.Bacc("TRN2", target_bir_lowering=False, num_devices=1)
    ins = [nc.dram_tensor("in_" + name, v.shape, mybir.dt.from_np(v.dtype), kind="ExternalInput").ap()
           for name, v in arrays.items()]
    out = nc.dram_tensor("out", (B, T, C), F32, kind="ExternalOutput").ap()
    build(nc, *ins, out)
    r = run_bass_kernel_spmd(nc, [{"in_" + name: v for name, v in arrays.items()}], core_ids=[0])
    return r.results[0]["out"]
```
